# Optimizing a Trainium2 kernel written in Bass

```python
import numpy as np
import jax
import jax.numpy as jnp

def _softmax(x, axis=-1):
    return jax.nn.softmax(x, axis=axis)

def _gelu(x):
    return jax.nn.gelu(x, approximate=True)

def _silu(x):
    return jax.nn.silu(x)

def _sigmoid(x):
    return jax.nn.sigmoid(x)

def _layernorm(x, axis=-1, eps=1e-05):
    m = jnp.mean(x, axis=axis, keepdims=True)
    v = jnp.var(x, axis=axis, keepdims=True)
    return (x - m) / jnp.sqrt(v + eps)

def _scatter_add(tgt, idx, src, axis=0):
    return tgt.at[idx].add(src)

def _segment_sum(src, seg, n):
    return jax.ops.segment_sum(src, seg, n)
kernel_name = 'mk_prb_d1_jaxref_r4_cd7f62'

def setup_inputs(seed: int=0):
    np.random.seed(seed)
    _w = jnp.asarray

    def _L0_attn_setup():
        import jax, jax.numpy as jnp
        import numpy as np
        B, T, C = (8, 1024, 256)
        LN_EPS = 1e-05
        NEG_INF = -1e+38

        def _ln(x, g, b):
            mu = jnp.mean(x, axis=-1, keepdims=True)
            var = jnp.mean(jnp.square(x - mu), axis=-1, keepdims=True)
            return (x - mu) * jax.lax.rsqrt(var + LN_EPS) * g + b

        def _shift(x):
            return jnp.concatenate([jnp.zeros_like(x[:, :1]), x[:, :-1]], axis=1)

        def _wkv(w, u, k, v):
            kt = jnp.moveaxis(k, 1, 0)
            vt = jnp.moveaxis(v, 1, 0)
            aa = jnp.zeros(k.shape[::2], k.dtype)
            bb = jnp.zeros(k.shape[::2], k.dtype)
            pp = jnp.full(k.shape[::2], NEG_INF, k.dtype)

            def step(carry, kv):
                aa, bb, pp = carry
                kk, vv = kv
                p = jnp.maximum(pp, u + kk)
                e1 = jnp.exp(pp - p)
                e2 = jnp.exp(u + kk - p)
                y = (e1 * aa + e2 * vv) / (e1 + e2)
                p2 = jnp.maximum(pp + w, w + kk)
                e1u = jnp.exp(pp + w - p2)
                e2u = jnp.exp(w + kk - p2)
                aa = e1u * aa + e2u * vv
                bb = e1u + e2u
                pp = p2 + jnp.log(bb)
                return ((aa, bb, pp), y)
            _, ys = jax.lax.scan(step, (aa, bb, pp), (kt, vt))
            return jnp.moveaxis(ys, 0, 1)
        key = jax.random.key(seed)
        ks = jax.random.split(key, 20)
        n = lambda i, sh, s=1.0: jax.random.normal(ks[i], sh, jnp.float32) * s
        un = lambda i, sh: jax.random.uniform(ks[i], sh, jnp.float32)
        return {'x': n(0, (B, T, C)), 'w': n(1, (C,), 0.01), 'u': n(2, (C,), 0.01), 'rk': un(3, (C,)), 'rv': un(4, (C,)), 'rr': un(5, (C,)), 'crk': un(6, (C,)), 'crr': un(7, (C,)), 'Wk': n(8, (C, C), 0.02), 'Wv': n(9, (C, C), 0.02), 'Wr': n(10, (C, C), 0.02), 'Wck': n(11, (4 * C, C), 0.02), 'Wcv': n(12, (C, 4 * C), 0.02), 'Wcr': n(13, (C, C), 0.02), 'ln1_g': jnp.ones((C,)), 'ln1_b': jnp.zeros((C,)), 'ln2_g': jnp.ones((C,)), 'ln2_b': jnp.zeros((C,))}
    _L0_attn_in = _L0_attn_setup()

    def _L0_ffn_setup():
        import jax, jax.numpy as jnp
        import numpy as np
        INT8_MAX = 127.0

        def _absmax_scale(x, axes):
            amax = jnp.max(jnp.abs(x), axis=axes, keepdims=True)
            return jnp.maximum(amax, 1e-12) / INT8_MAX
        key = jax.random.key(seed)
        k1, k2 = jax.random.split(key)
        lhs = jax.random.normal(k1, (4, 2048, 256), dtype=jnp.float32)
        rhs = jax.random.normal(k2, (256, 256), dtype=jnp.float32)
        return {'lhs': lhs, 'rhs': rhs}
    _L0_ffn_in = _L0_ffn_setup()
    _d = {'L0_attn_x': _L0_attn_in['x'], 'L0_attn_w': _L0_attn_in['w'], 'L0_attn_u': _L0_attn_in['u'], 'L0_attn_rk': _L0_attn_in['rk'], 'L0_attn_rv': _L0_attn_in['rv'], 'L0_attn_rr': _L0_attn_in['rr'], 'L0_attn_crk': _L0_attn_in['crk'], 'L0_attn_crr': _L0_attn_in['crr'], 'L0_attn_Wk': _L0_attn_in['Wk'], 'L0_attn_Wv': _L0_attn_in['Wv'], 'L0_attn_Wr': _L0_attn_in['Wr'], 'L0_attn_Wck': _L0_attn_in['Wck'], 'L0_attn_Wcv': _L0_attn_in['Wcv'], 'L0_attn_Wcr': _L0_attn_in['Wcr'], 'L0_attn_ln1_g': _L0_attn_in['ln1_g'], 'L0_attn_ln1_b': _L0_attn_in['ln1_b'], 'L0_attn_ln2_g': _L0_attn_in['ln2_g'], 'L0_attn_ln2_b': _L0_attn_in['ln2_b'], 'L0_ffn_rhs': _L0_ffn_in['rhs']}
    _x0 = _d['L0_attn_x']
    _d['L0_attn_x'] = jax.random.normal(jax.random.fold_in(jax.random.key(seed), 1), (4, 2048, 256), dtype=_x0.dtype)
    del _x0
    return _d

def reference(L0_attn_x, L0_attn_w, L0_attn_u, L0_attn_rk, L0_attn_rv, L0_attn_rr, L0_attn_crk, L0_attn_crr, L0_attn_Wk, L0_attn_Wv, L0_attn_Wr, L0_attn_Wck, L0_attn_Wcv, L0_attn_Wcr, L0_attn_ln1_g, L0_attn_ln1_b, L0_attn_ln2_g, L0_attn_ln2_b, L0_ffn_rhs):

    def _L0_attn_ref(x, w, u, rk, rv, rr, crk, crr, Wk, Wv, Wr, Wck, Wcv, Wcr, ln1_g, ln1_b, ln2_g, ln2_b):
        import jax, jax.numpy as jnp
        import numpy as np
        B, T, C = (8, 1024, 256)
        LN_EPS = 1e-05
        NEG_INF = -1e+38

        def _ln(x, g, b):
            mu = jnp.mean(x, axis=-1, keepdims=True)
            var = jnp.mean(jnp.square(x - mu), axis=-1, keepdims=True)
            return (x - mu) * jax.lax.rsqrt(var + LN_EPS) * g + b

        def _shift(x):
            return jnp.concatenate([jnp.zeros_like(x[:, :1]), x[:, :-1]], axis=1)

        def _wkv(w, u, k, v):
            kt = jnp.moveaxis(k, 1, 0)
            vt = jnp.moveaxis(v, 1, 0)
            aa = jnp.zeros(k.shape[::2], k.dtype)
            bb = jnp.zeros(k.shape[::2], k.dtype)
            pp = jnp.full(k.shape[::2], NEG_INF, k.dtype)

            def step(carry, kv):
                aa, bb, pp = carry
                kk, vv = kv
                p = jnp.maximum(pp, u + kk)
                e1 = jnp.exp(pp - p)
                e2 = jnp.exp(u + kk - p)
                y = (e1 * aa + e2 * vv) / (e1 + e2)
                p2 = jnp.maximum(pp + w, w + kk)
                e1u = jnp.exp(pp + w - p2)
                e2u = jnp.exp(w + kk - p2)
                aa = e1u * aa + e2u * vv
                bb = e1u + e2u
                pp = p2 + jnp.log(bb)
                return ((aa, bb, pp), y)
            _, ys = jax.lax.scan(step, (aa, bb, pp), (kt, vt))
            return jnp.moveaxis(ys, 0, 1)
        xa = _ln(x, ln1_g, ln1_b)
        xp = _shift(xa)
        xk = xa * rk + xp * (1.0 - rk)
        xv = xa * rv + xp * (1.0 - rv)
        xr = xa * rr + xp * (1.0 - rr)
        k = jnp.einsum('btc,dc->btd', xk, Wk)
        v = jnp.einsum('btc,dc->btd', xv, Wv)
        r = jnp.einsum('btc,dc->btd', xr, Wr)
        wkv = _wkv(w, u, k, v)
        x1 = x + jax.nn.sigmoid(r) * wkv
        xb = _ln(x1, ln2_g, ln2_b)
        xpb = _shift(xb)
        xck = xb * crk + xpb * (1.0 - crk)
        xcr = xb * crr + xpb * (1.0 - crr)
        kc = jnp.square(jax.nn.relu(jnp.einsum('btc,dc->btd', xck, Wck)))
        vc = jnp.einsum('bth,dh->btd', kc, Wcv)
        out = x1 + jax.nn.sigmoid(jnp.einsum('btc,dc->btd', xcr, Wcr)) * vc
        return out

    def _L0_ffn_ref(lhs, rhs):
        import jax, jax.numpy as jnp
        import numpy as np
        INT8_MAX = 127.0

        def _absmax_scale(x, axes):
            amax = jnp.max(jnp.abs(x), axis=axes, keepdims=True)
            return jnp.maximum(amax, 1e-12) / INT8_MAX
        lhs_scale = _absmax_scale(lhs, (2,))
        rhs_scale = _absmax_scale(rhs, (0,))
        q_lhs = jnp.clip(jnp.round(lhs / lhs_scale), -INT8_MAX, INT8_MAX).astype(jnp.int8)
        q_rhs = jnp.clip(jnp.round(rhs / rhs_scale), -INT8_MAX, INT8_MAX).astype(jnp.int8)
        acc = jax.lax.dot_general(q_lhs, q_rhs, (((2,), (0,)), ((), ())), preferred_element_type=jnp.int32)
        return acc.astype(jnp.float32) * lhs_scale * rhs_scale
    x = L0_attn_x
    xn = _layernorm(x, axis=-1)
    x = x + _L0_attn_ref(xn, L0_attn_w, L0_attn_u, L0_attn_rk, L0_attn_rv, L0_attn_rr, L0_attn_crk, L0_attn_crr, L0_attn_Wk, L0_attn_Wv, L0_attn_Wr, L0_attn_Wck, L0_attn_Wcv, L0_attn_Wcr, L0_attn_ln1_g, L0_attn_ln1_b, L0_attn_ln2_g, L0_attn_ln2_b) + _L0_ffn_ref(xn, L0_ffn_rhs)
    return x

_drawn_inputs = setup_inputs


def setup_inputs(seed=0):
    import zlib

    import numpy as np

    out = dict(_drawn_inputs(seed))
    spreads = {'L0_attn_ln1_g': (1.0, 0.6),
     'L0_attn_ln1_b': (0.0, 0.672),
     'L0_attn_ln2_g': (1.0, 0.6),
     'L0_attn_ln2_b': (0.0, 0.8)}
    factors = {'L0_attn_w': 8.0,
     'L0_attn_u': 64.0,
     'L0_attn_rk': 8.0,
     'L0_attn_rv': 8.0,
     'L0_attn_rr': 8.0,
     'L0_attn_crk': 8.0,
     'L0_attn_crr': 8.0,
     'L0_attn_Wk': 8.0,
     'L0_attn_Wv': 3.071,
     'L0_attn_Wr': 8.0,
     'L0_attn_Wck': 8.0,
     'L0_attn_Wcv': 8.0,
     'L0_attn_Wcr': 8.0,
     'L0_ffn_rhs': 4.699}
    for name, (base, spread) in spreads.items():
        noise = np.random.default_rng([zlib.crc32(name.encode()), seed]).standard_normal(out[name].shape)
        drawn = base * np.exp(spread * noise) if base else spread * noise
        out[name] = jnp.asarray(drawn.astype(out[name].dtype))
    for name, factor in factors.items():
        out[name] = (out[name] * factor).astype(out[name].dtype)
    return out
```

```python
from contextlib import ExitStack

import concourse.bass as bass
from concourse import mybir

P = 128
B, T, C, H = 4, 2048, 256, 1024
N = T // P
HALF = C // P
HT = H // P
SEG = HALF * B
W = B * P
RING = 4
KC = 4

F32 = mybir.dt.float32
BF16 = mybir.dt.bfloat16
I32 = mybir.dt.int32
ALU = mybir.AluOpType
ACT = mybir.ActivationFunctionType
AX = mybir.AxisListType

EPS = 1e-5
NEG_INF = -1e38
BIG = 3e38
INT8_MAX = 127.0
MAGIC = 1.5 * 2.0**23

COLS = ["g1", "b1", "rk", "rv", "rr", "g2", "b2", "crk", "crr", "w", "u"]


def rwkv_program(nc, x, cols, wk, wv, wr, wcr, wck, wcv, rhs, out):
    ctx = ExitStack()
    with ctx:
        def sb(name, shape, dt=F32):
            return ctx.enter_context(nc.sbuf_tensor(name, shape, dt))

        def psum(name, shape, dt=F32):
            return ctx.enter_context(nc.psum_tensor(name, shape, dt))

        def sem(name):
            return ctx.enter_context(nc.semaphore(name))

        wk_s, wv_s, wr_s, wcr_s = (sb(n, [P, HALF, C]) for n in ("wk_s", "wv_s", "wr_s", "wcr_s"))
        wck_s = sb("wck_s", [P, HALF, H])
        wcv_s = sb("wcv_s", [P, HT, C])
        rhs_s = sb("rhs_s", [P, HALF, C])
        cols_s = sb("cols_s", [P, len(COLS), HALF])
        ident = sb("ident", [P, P])
        ident_b = sb("ident_b", [P, P], BF16)
        ones = sb("ones", [P, P])
        steps_i = sb("steps_i", [P, P], I32)
        steps_f = sb("steps_f", [P, P])
        ramp = sb("ramp", [P, HALF, P])
        ramp_end = sb("ramp_end", [P, SEG, 1])
        half_u = sb("half_u", [P, HALF])
        keep = sb("keep", [P, SEG, P + 1], BF16)
        zeros = sb("zeros", [P, SEG, 1])
        count = sb("count", [P, 2])
        neg_half = sb("neg_half", [P, 8])
        rhs_q = sb("rhs_q", [P, HALF, C], BF16)
        rhs_scale = sb("rhs_scale", [P, C])
        rq_amax = sb("rq_amax", [P, HALF])
        rq_scale = sb("rq_scale", [P, HALF])
        rq_inv = sb("rq_inv", [P, HALF])

        x_t = [sb(f"x_t{i}", [P, B, C]) for i in range(2)]
        xn = [sb(f"xn{i}", [P, B, C]) for i in range(2)]
        nrm = sb("nrm", [P, B, C])
        q_f = sb("q_f", [P, B, C])
        q_b = sb("q_b", [P, B, C], BF16)
        base0 = [sb(f"base0_{i}", [P, B, C]) for i in range(2)]
        base1 = [sb(f"base1_{i}", [P, B, C]) for i in range(2)]
        st1, st2 = sb("st1", [P, B, 6]), sb("st2", [P, B, 6])
        mv1, mv2 = sb("mv1", [P, B, 2]), sb("mv2", [P, B, 2])
        pw1, rsq1 = sb("pw1", [P, 8]), sb("rsq1", [P, 8])
        rcp1 = sb("rcp1", [P, B])
        pw2, rsq2 = sb("pw2", [P, B]), sb("rsq2", [P, B])
        scale_z, bias_z = sb("scale_z", [P, B]), sb("bias_z", [P, B])
        bias_2 = sb("bias_2", [P, B])
        amax, lhs_scale, lhs_inv = sb("amax", [P, B]), sb("lhs_scale", [P, B]), sb("lhs_inv", [P, B])

        q_c = sb("q_c", [P, HALF, W], BF16)
        xa = [sb(f"xa{i}", [P, SEG, P + 1]) for i in range(2)]
        xb = [sb(f"xb{i}", [P, SEG, P + 1]) for i in range(2)]
        dx = sb("dx", [P, SEG, P])
        dxb = sb("dxb", [P, SEG, P])
        xk, xv, xr = (sb(n, [P, HALF, W]) for n in ("xk", "xv", "xr"))
        xck, xcr = sb("xck", [P, HALF, W]), sb("xcr", [P, HALF, W])
        kt = sb("kt", [P, SEG, P + 1])
        mx = sb("mx", [P, SEG, P + 1])
        dd = sb("dd", [P, SEG, P])
        decay = sb("decay", [P, SEG, P + 1])
        inject = sb("inject", [P, SEG, P + 1])
        ss = sb("ss", [P, SEG, P + 1])
        aa = sb("aa", [P, SEG, P + 1])
        tg = sb("tg", [P, SEG, P])
        vs = sb("vs", [P, HALF, W])
        tr = sb("tr", [P, HALF, W])
        yz = sb("yz", [P, HALF, W])
        tc = sb("tc", [P, HALF, W])
        z2 = sb("z2", [P, HALF, W])
        relu_h = [sb(f"relu_h{i}", [P, W]) for i in range(2)]
        kc = [sb(f"kc{i}", [P, W]) for i in range(KC)]

        ring = psum("ring", [P, RING, W])
        turn = psum("turn", [P, HALF, W])
        vc = psum("vc", [P, HALF, W])

        x_in = [sem("x_in0"), sem("x_in1")]
        stored = [sem("stored0"), sem("stored1")]
        cols_in, rhs_in = sem("cols_in"), sem("rhs_in")
        kvr_in, cm_in = sem("kvr_in"), sem("cm_in")
        consts_pool, ident_pool, setup_dve, setup_pe = sem("consts_pool"), sem("ident_pool"), sem("setup_dve"), sem("setup_pe")
        ln1_step, ln2_step = sem("ln1_step"), sem("ln2_step")
        rsq1_ok, rsq2_ok = sem("rsq1_ok"), sem("rsq2_ok")
        xz_scales, xz_ok, xn_ok, quant_scales = sem("xz_scales"), sem("xz_ok"), sem("xn_ok"), sem("quant_scales")
        qf_ok, qb_ok, qc_ok, ffn_ok, base0_ok = sem("qf_ok"), sem("qb_ok"), sem("qc_ok"), sem("ffn_ok"), sem("base0_ok")
        t1_done, tq_done, ff_done = sem("t1_done"), sem("tq_done"), sem("ff_done")
        t2_done, t3_done, t4_done = sem("t2_done"), sem("t3_done"), sem("t4_done")
        xa_ok, xa_carry, dx_ok, xk_ok, xv_ok, xr_ok = (sem(n) for n in ("xa_ok", "xa_carry", "dx_ok", "xk_ok", "xv_ok", "xr_ok"))
        k_done, v_done, r_done = sem("k_done"), sem("v_done"), sem("r_done")
        kt_ok, kt_carry, vs_ok, tr_ok = sem("kt_ok"), sem("kt_carry"), sem("vs_ok"), sem("tr_ok")
        mx_ok, d0_ok, relu_d, em_ok, ek_ok = sem("mx_ok"), sem("d0_ok"), sem("relu_d"), sem("em_ok"), sem("ek_ok")
        s_carry, ss_ok, ln_ok, d_ok = sem("s_carry"), sem("ss_ok"), sem("ln_ok"), sem("d_ok")
        relu_e, e1_ok, e2_ok, tg_ok = sem("relu_e"), sem("e1_ok"), sem("e2_ok"), sem("tg_ok")
        aa_carry, ev_ok, aa_ok, y_step, z_ok = sem("aa_carry"), sem("ev_ok"), sem("aa_ok"), sem("y_step"), sem("z_ok")
        x1_ok, bias2_ok, xbt_ok, xb_ok, xb_carry, dxb_ok = (sem(n) for n in ("x1_ok", "bias2_ok", "xbt_ok", "xb_ok", "xb_carry", "dxb_ok"))
        xck_ok, xcr_ok, rc_done, tc_ok = sem("xck_ok"), sem("xcr_ok"), sem("rc_done"), sem("tc_ok")
        h_done, relu_ok, kc_ok, vc_step = sem("h_done"), sem("relu_ok"), sem("kc_ok"), sem("vc_step")
        z2_ok, base1_ok, out_ok = sem("z2_ok"), sem("base1_ok"), sem("out_ok")

        def back(t, k):
            d = t[1] - k
            return t[0] + d // 2, d % 2

        def known(c):
            return isinstance(c[0], int)

        def exists(c):
            return not known(c) or 0 <= 2 * c[0] + c[1] < N

        def reached(eng, s, c, per=1, k=None):
            k = per - 1 if k is None else k
            n = 2 * c[0] + c[1]
            if known(c):
                if n < 0:
                    return
                n = min(n, N - 1)
            eng.wait_ge(s, n * per + k + 1)

        def reached_dma(eng, sems, c):
            if known(c) and c[0] < 0:
                return
            eng.wait_ge(sems[c[1]], (c[0] + 1) * 16)

        def iterations(eng, step):
            for t in range(4):
                step((t // 2, t % 2))
            with eng.Fori(2, N // 2) as m:
                step((m, 0))
                step((m, 1))
            for t in range(N, N + 2):
                step((t // 2, t % 2))

        def col(name, h):
            i = COLS.index(name)
            return cols_s[:, i, h:h + 1]

        def half(tile, h, a=0, b=P):
            return tile[:, B * h:B * (h + 1), a:b]

        def seg(ap):
            return ap.rearrange("p (b j) -> p b j", b=B)

        x_d = x.rearrange("b (n p) c -> n p b c", p=P)
        out_d = out.rearrange("b (n p) c -> n p b c", p=P)

        block = ctx.enter_context(nc.Block())

        @block.sync
        def _(sp):
            def load(c):
                sp.dma_start(x_t[c[1]][:], x_d[2 * c[0] + c[1]]).then_inc(x_in[c[1]], 16)

            load((0, 0))
            sp.dma_start(cols_s[:], cols.rearrange("p (i h) -> p i h", h=HALF)).then_inc(cols_in, 16)
            load((0, 1))
            for w_d, w_s in ((wk, wk_s), (wv, wv_s), (wr, wr_s)):
                sp.dma_start(w_s[:], w_d.rearrange("(h p) d -> p h d", p=P)).then_inc(kvr_in, 16)

            def step(t):
                c = back(t, 2)
                if exists(c):
                    reached(sp, out_ok, c)
                    sp.dma_start(out_d[2 * c[0] + c[1]], base1[c[1]][:]).then_inc(stored[c[1]], 16)
                ahead = back(t, -1)
                if exists(ahead) and not (known(ahead) and 2 * ahead[0] + ahead[1] < 2):
                    reached(sp, base0_ok, back(ahead, 2))
                    load(ahead)

            for t in range(4):
                step((t // 2, t % 2))
            with sp.Fori(2, N // 2 - 1) as m:
                step((m, 0))
                step((m, 1))
            for t in range(N - 2, N + 2):
                step((t // 2, t % 2))
            sp.wait_ge(stored[0], 16 * (N // 2))
            sp.wait_ge(stored[1], 16 * (N // 2))

        @block.gpsimd
        def _(pool):
            pool.memset(ones[:], 1.0).then_inc(ident_pool, 1)
            pool.memset(neg_half[:], -0.5).then_inc(ident_pool, 1)
            pool.wait_ge(ident_pool, 2)
            pool.affine_select(out=ident[:], in_=ones[:], compare_op=ALU.is_equal, fill=0.0, base=0,
                               pattern=[[-1, P]], channel_multiplier=1).then_inc(ident_pool, 1)
            pool.iota(steps_i[:], pattern=[[1, P]], base=0, channel_multiplier=0).then_inc(ident_pool, 1)
            pool.memset(xa[1][:, :, P:P + 1], 0.0).then_inc(consts_pool, 1)
            pool.memset(xb[1][:, :, P:P + 1], 0.0).then_inc(consts_pool, 1)
            pool.memset(mx[:, :, P:P + 1], NEG_INF).then_inc(consts_pool, 1)
            pool.memset(ss[:, :, P:P + 1], 1.0).then_inc(consts_pool, 1)
            pool.memset(aa[:, :, P:P + 1], 0.0).then_inc(consts_pool, 1)
            pool.memset(decay[:, :, 0:1], 0.0).then_inc(consts_pool, 1)
            pool.memset(keep[:, :, 1:P + 1], BIG).then_inc(consts_pool, 1)
            pool.memset(keep[:, :, 0:1], -BIG).then_inc(consts_pool, 1)
            pool.memset(zeros[:], 0.0).then_inc(consts_pool, 1)
            pool.wait_ge(consts_pool, 9)

            def step(t):
                a, b = t, back(t, 1)
                if exists(a):
                    reached(pool, ln1_step, a, 6)
                    pool.tensor_tensor(rsq1[:], pw1[:], neg_half[:], ALU.pow).then_inc(rsq1_ok, 1)
                    reached(pool, xr_ok, back(a, 2))
                    reached(pool, xa_ok, back(a, 1), 2)
                    pool.tensor_tensor(xa[a[1]][:, :, 0:1], xa[1 - a[1]][:, :, P:P + 1], zeros[:], ALU.add).then_inc(xa_carry, 1)
                    reached(pool, xa_ok, a, 2)
                    reached(pool, xa_carry, a)
                    reached(pool, xr_ok, back(a, 1))
                    pool.tensor_tensor(dx[:], xa[a[1]][:, :, 1:P + 1], xa[a[1]][:, :, 0:P],
                                       ALU.subtract).then_inc(dx_ok, 1)
                    reached(pool, ffn_ok, a)
                    reached_dma(pool, x_in, a)
                    pool.tensor_tensor(base0[a[1]][:], base0[a[1]][:], x_t[a[1]][:], ALU.add).then_inc(base0_ok, 1)
                if exists(b):
                    reached(pool, xck_ok, back(b, 2))
                    reached(pool, xb_ok, back(b, 1), 2)
                    pool.tensor_tensor(xb[b[1]][:, :, 0:1], xb[1 - b[1]][:, :, P:P + 1], zeros[:], ALU.add).then_inc(xb_carry, 1)
                    reached(pool, ln2_step, b, 3)
                    pool.tensor_tensor(rsq2[:], pw2[:], neg_half[:, 0:B], ALU.pow).then_inc(rsq2_ok, 1)
                    reached(pool, base0_ok, b)
                    reached_dma(pool, stored, back(b, 2))
                    pool.tensor_tensor(base1[b[1]][:], base0[b[1]][:], xn[b[1]][:], ALU.add).then_inc(base1_ok, 1)

            iterations(pool, step)

        @block.scalar
        def _(act):
            act.dma_start(rhs_s[:], rhs.rearrange("(h p) d -> p h d", p=P)).then_inc(rhs_in, 16)
            for w_d, w_s in ((wcr, wcr_s), (wck, wck_s), (wcv, wcv_s)):
                act.dma_start(w_s[:], w_d.rearrange("(h p) d -> p h d", p=P)).then_inc(cm_in, 16)
            act.wait_ge(setup_dve, 8)
            act.wait_ge(consts_pool, 9)

            def gate_c(c):
                for h in range(HALF):
                    reached(act, rc_done, c, HALF, h)
                    if h == 0:
                        reached(act, z2_ok, back(c, 1))
                    act.activation(tc[:, h, :], ring[:, h, :], ACT.Tanh, scale=0.5).then_inc(tc_ok, 1)

            def hidden(c, j):
                reached(act, h_done, c, HT, j)
                reached(act, kc_ok, c if j >= 2 else back(c, 1), HT, (j - 2) % HT)
                act.activation(relu_h[j % 2][:], ring[:, (2 + j) % RING, :], ACT.Relu).then_inc(relu_ok, 1)
                reached(act, relu_ok, c, HT, j)
                reached(act, vc_step, c if j >= KC else back(c, 1), HT, (j - KC) % HT)
                act.activation(kc[j % KC][:], relu_h[j % 2][:], ACT.Square).then_inc(kc_ok, 1)

            def norm_z(a):
                reached(act, xz_scales, a, 2)
                reached(act, t3_done, back(a, 2))
                if known(a):
                    reached(act, t1_done, back(a, 1))
                for b in range(B):
                    i = act.activation(nrm[:, b, :], x_t[a[1]][:, b, :], ACT.Identity,
                                       scale=scale_z[:, b:b + 1], bias=bias_z[:, b:b + 1])
                i.then_inc(xz_ok, 1)

            def exps(c, ready, relus, low_ok, high_ok):
                reached(act, ready, c)
                act.activation(decay[:, :, 1:P + 1], dd[:], ACT.Relu).then_inc(relus, 1)
                act.activation(inject[:, :, 1:P + 1], dd[:], ACT.Relu, scale=-1.0).then_inc(relus, 1)
                reached(act, relus, c, 2, 0)
                act.activation(decay[:, :, 1:P + 1], decay[:, :, 1:P + 1], ACT.Exp, scale=-1.0).then_inc(low_ok, 1)
                reached(act, relus, c, 2, 1)
                act.activation(inject[:, :, 1:P + 1], inject[:, :, 1:P + 1], ACT.Exp, scale=-1.0).then_inc(high_ok, 1)

            def quant(a):
                reached(act, quant_scales, a, 3)
                reached(act, qb_ok, back(a, 1))
                for b in range(B):
                    i = act.activation(q_f[:, b, :], xn[a[1]][:, b, :], ACT.Copy, scale=lhs_inv[:, b:b + 1], bias=MAGIC)
                i.then_inc(qf_ok, 1)

            def evac_xa(a):
                reached(act, t1_done, a)
                reached(act, xr_ok, back(a, 2))
                reached(act, xa_carry, back(a, 1))
                for h in range(HALF):
                    act.activation(half(xa[a[1]], h, 1, P + 1), seg(turn[:, h, :]), ACT.Identity,
                                   scale=col("g1", h), bias=col("b1", h)).then_inc(xa_ok, 1)

            def evac_xb(b):
                reached(act, t3_done, b)
                reached(act, xck_ok, back(b, 2))
                reached(act, xb_carry, back(b, 1))
                for h in range(HALF):
                    act.activation(half(xb[b[1]], h, 1, P + 1), seg(turn[:, h, :]), ACT.Identity,
                                   scale=col("g2", h), bias=col("b2", h)).then_inc(xb_ok, 1)

            def step(t):
                a, b, c = t, back(t, 1), back(t, 2)
                if exists(c):
                    gate_c(c)
                    hidden(c, 0)
                if exists(a):
                    norm_z(a)
                if exists(c):
                    hidden(c, 1)
                if exists(b):
                    exps(b, d0_ok, relu_d, em_ok, ek_ok)
                if exists(c):
                    hidden(c, 2)
                if exists(a):
                    quant(a)
                if exists(c):
                    hidden(c, 3)
                if exists(b):
                    reached(act, ss_ok, b)
                    act.activation(kt[:, :, 0:P], ss[:, :, 0:P], ACT.Ln).then_inc(ln_ok, 1)
                if exists(a):
                    evac_xa(a)
                if exists(c):
                    hidden(c, 4)
                if exists(b):
                    exps(b, d_ok, relu_e, e1_ok, e2_ok)
                if exists(c):
                    hidden(c, 5)
                if exists(b):
                    reached(act, z_ok, back(b, 1))
                    for h in range(HALF):
                        i = act.activation(half(tg, h), half(dd, h), ACT.Tanh, scale=0.5, bias=half_u[:, h:h + 1])
                    i.then_inc(tg_ok, 1)
                if exists(c):
                    hidden(c, 6)
                    hidden(c, 7)
                if exists(b):
                    reached(act, bias2_ok, b)
                    reached(act, t1_done, a)
                    for s in range(B):
                        i = act.activation(nrm[:, s, :], xn[b[1]][:, s, :], ACT.Identity,
                                           scale=rsq2[:, s:s + 1], bias=bias_2[:, s:s + 1])
                    i.then_inc(xbt_ok, 1)
                if exists(a):
                    reached(act, y_step, b, 3, 0)
                    for h in range(HALF):
                        reached(act, v_done, a, HALF, h)
                        act.activation(vs[:, h, :], ring[:, (12 + h) % RING, :], ACT.Copy).then_inc(vs_ok, 1)
                if exists(b):
                    evac_xb(b)
                if exists(a):
                    reached(act, z_ok, b)
                    for h in range(HALF):
                        reached(act, r_done, a, HALF, h)
                        act.activation(tr[:, h, :], ring[:, (14 + h) % RING, :], ACT.Tanh, scale=0.5).then_inc(tr_ok, 1)

            iterations(act, step)

        @block.vector
        def _(dve):
            dve.wait_ge(ident_pool, 4)
            dve.wait_ge(cols_in, 16)
            dve.tensor_copy(ident_b[:], ident[:]).then_inc(setup_dve, 1)
            dve.tensor_copy(steps_f[:], steps_i[:]).then_inc(setup_dve, 1)
            dve.wait_ge(setup_dve, 2)
            for h in range(HALF):
                dve.tensor_scalar(ramp[:, h, :], steps_f[:], col("w", h), None, ALU.mult)
                dve.tensor_scalar(ramp_end[:, B * h:B * (h + 1), :], ones[:, 0:B].unsqueeze(2), col("w", h), float(P),
                                  ALU.mult, ALU.mult).then_inc(setup_dve, 1)
            dve.tensor_scalar(half_u[:], cols_s[:, COLS.index("u"), :], 0.5, None, ALU.mult).then_inc(setup_dve, 1)
            dve.wait_ge(setup_pe, 1)
            dve.tensor_reduce(rq_amax[:], turn[:, :, 0:C], AX.X, ALU.max,
                              apply_absolute_value=True).then_inc(setup_dve, 1)
            dve.wait_ge(setup_dve, 6)
            dve.tensor_scalar(rq_scale[:], rq_amax[:], 1e-12, 1.0 / INT8_MAX, ALU.max, ALU.mult).then_inc(setup_dve, 1)
            dve.wait_ge(setup_dve, 7)
            dve.reciprocal(rq_inv[:], rq_scale[:]).then_inc(setup_dve, 1)
            dve.wait_ge(setup_dve, 8)
            for h in range(HALF):
                dve.tensor_scalar(q_f[:, h, :], turn[:, h, 0:C], rq_inv[:, h:h + 1], MAGIC, ALU.mult, ALU.add)
                dve.tensor_scalar(xn[0][:, h, 0:P], ident[:], rq_scale[:, h:h + 1], None, ALU.mult).then_inc(setup_dve, 1)
            dve.wait_ge(setup_dve, 10)
            dve.tensor_scalar(q_b[:, 0:HALF, :], q_f[:, 0:HALF, :], MAGIC + INT8_MAX, MAGIC,
                              ALU.min, ALU.subtract).then_inc(setup_dve, 1)
            dve.wait_ge(setup_pe, 2)
            dve.tensor_scalar(rhs_q[:], turn[:, 0, :].bitcast(BF16)[:, 0:HALF * C].rearrange("p (h d) -> p h d", h=HALF),
                              -INT8_MAX, None, ALU.max).then_inc(setup_dve, 1)
            dve.tensor_copy(rhs_scale[:], vc[:, 0, 0:C]).then_inc(setup_dve, 1)
            dve.wait_ge(consts_pool, 9)
            dve.wait_ge(setup_dve, 13)

            def stats(tile, st, mv, steps, c, per):
                for s in range(B):
                    i = dve.bn_stats(st[:, s, :], tile[:, s, :])
                i.then_inc(steps, 1)
                reached(dve, steps, c, per, 0)
                dve.tensor_copy(count[:, 0:1], st[:, 0, 0:1])
                for s in range(B):
                    i = dve.bn_aggr(mv[:, s, :], st[:, s, :])
                i.then_inc(steps, 1)
                reached(dve, steps, c, per, 1)

            def norm1_stats(a):
                reached_dma(dve, x_in, a)
                stats(x_t[a[1]], st1, mv1, ln1_step, a, 6)
                dve.tensor_scalar(pw1[:, 0:B], mv1[:, :, 1], EPS, None, ALU.add).then_inc(ln1_step, 1)
                reached(dve, ln1_step, a, 6, 2)
                dve.reciprocal(rcp1[:], pw1[:, 0:B]).then_inc(ln1_step, 1)
                reached(dve, ln1_step, a, 6, 3)
                dve.tensor_tensor(rcp1[:], mv1[:, :, 1], rcp1[:], ALU.mult).then_inc(ln1_step, 1)
                reached(dve, ln1_step, a, 6, 4)
                dve.tensor_scalar(pw1[:, B:2 * B], rcp1[:], EPS, None, ALU.add).then_inc(ln1_step, 1)

            def running_max(b):
                dve.tensor_tensor(kt[:, :, 0:1], mx[:, :, P:P + 1], ramp_end[:], ALU.add).then_inc(kt_carry, 1)
                reached(dve, kt_ok, b, HALF)
                reached(dve, kt_carry, b)
                dve.tensor_tensor_scan(mx[:].rearrange("p s j -> p (s j)"), keep[:].rearrange("p s j -> p (s j)"),
                                       kt[:].rearrange("p s j -> p (s j)"), 0.0, ALU.min, ALU.max).then_inc(mx_ok, 1)
                reached(dve, mx_ok, b)
                dve.tensor_tensor(dd[:], kt[:, :, 1:P + 1], mx[:, :, 0:P], ALU.subtract).then_inc(d0_ok, 1)

            def norm1(a):
                reached(dve, rsq1_ok, a)
                dve.tensor_tensor(scale_z[:], rsq1[:, 0:B], rsq1[:, B:2 * B], ALU.mult).then_inc(xz_scales, 1)
                reached(dve, xz_scales, a, 2, 0)
                dve.scalar_tensor_tensor(bias_z[:], mv1[:, :, 0], -1.0, scale_z[:], ALU.mult,
                                         ALU.mult).then_inc(xz_scales, 1)
                reached(dve, base1_ok, back(a, 2))
                reached(dve, xbt_ok, back(a, 2))
                for s in range(B):
                    i = dve.tensor_scalar(xn[a[1]][:, s, :], x_t[a[1]][:, s, :], mv1[:, s, 0:1], rsq1[:, s:s + 1],
                                          ALU.subtract, ALU.mult)
                i.then_inc(xn_ok, 1)
                reached(dve, xn_ok, a)
                dve.tensor_reduce(amax[:], xn[a[1]][:], AX.X, ALU.max, apply_absolute_value=True).then_inc(quant_scales, 1)
                reached(dve, quant_scales, a, 3, 0)
                dve.tensor_scalar(lhs_scale[:], amax[:], 1e-12, 1.0 / INT8_MAX, ALU.max, ALU.mult).then_inc(quant_scales, 1)
                reached(dve, quant_scales, a, 3, 1)
                dve.reciprocal(lhs_inv[:], lhs_scale[:]).then_inc(quant_scales, 1)

            def scan_s(b):
                reached(dve, em_ok, b)
                reached(dve, ek_ok, b)
                dve.tensor_copy(inject[:, :, 0:1], ss[:, :, P:P + 1]).then_inc(s_carry, 1)
                reached(dve, s_carry, b)
                dve.tensor_tensor_scan(ss[:].rearrange("p s j -> p (s j)"), decay[:].rearrange("p s j -> p (s j)"),
                                       inject[:].rearrange("p s j -> p (s j)"), 0.0, ALU.mult, ALU.add).then_inc(ss_ok, 1)

            def round_q(a):
                reached(dve, qf_ok, a)
                reached(dve, tq_done, back(a, 1))
                dve.tensor_scalar(q_b[:], q_f[:], MAGIC + INT8_MAX, MAGIC, ALU.min, ALU.subtract).then_inc(qb_ok, 1)

            def log_ratio(b):
                reached(dve, ln_ok, b)
                dve.tensor_tensor(dd[:], dd[:], kt[:, :, 0:P], ALU.subtract).then_inc(d_ok, 1)

            def evac_q(a):
                reached(dve, tq_done, a)
                reached(dve, ff_done, back(a, 1))
                dve.tensor_scalar(q_c[:], turn[:, 0, :].bitcast(BF16).rearrange("p (h w) -> p h w", h=HALF),
                                  -INT8_MAX, None, ALU.max).then_inc(qc_ok, 1)

            def token_mix(a):
                reached(dve, dx_ok, a)
                for name, tile, done, ok in (("rk", xk, k_done, xk_ok), ("rv", xv, v_done, xv_ok), ("rr", xr, r_done, xr_ok)):
                    reached(dve, done, back(a, 1), HALF)
                    for h in range(HALF):
                        i = dve.scalar_tensor_tensor(seg(tile[:, h, :]), half(dx, h), col(name, h), half(xa[a[1]], h),
                                                     ALU.mult, ALU.add)
                    i.then_inc(ok, 1)

            def scan_aa(b):
                reached(dve, e2_ok, b)
                reached(dve, vs_ok, b, HALF)
                dve.tensor_copy(inject[:, :, 0:1], aa[:, :, P:P + 1]).then_inc(aa_carry, 1)
                dve.tensor_tensor(inject[:, :, 1:P + 1], inject[:, :, 1:P + 1],
                                  vs[:].rearrange("p h (b j) -> p (h b) j", b=B), ALU.mult).then_inc(ev_ok, 1)
                reached(dve, aa_carry, b)
                reached(dve, ev_ok, b)
                reached(dve, e1_ok, b)
                dve.tensor_tensor_scan(aa[:].rearrange("p s j -> p (s j)"), decay[:].rearrange("p s j -> p (s j)"),
                                       inject[:].rearrange("p s j -> p (s j)"), 0.0, ALU.mult, ALU.add).then_inc(aa_ok, 1)

            def gated(b):
                y = yz[:].rearrange("p h (b j) -> p (h b) j", b=B)
                reached(dve, aa_ok, b)
                reached(dve, t2_done, back(b, 1))
                dve.tensor_tensor(y, vs[:].rearrange("p h (b j) -> p (h b) j", b=B), aa[:, :, 0:P],
                                  ALU.subtract).then_inc(y_step, 1)
                reached(dve, y_step, b, 3, 0)
                reached(dve, tg_ok, b)
                dve.scalar_tensor_tensor(y, tg[:], 1.0, y, ALU.add, ALU.mult).then_inc(y_step, 1)
                reached(dve, y_step, b, 3, 1)
                dve.scalar_tensor_tensor(y, aa[:, :, 0:P], 2.0, y, ALU.mult, ALU.add).then_inc(y_step, 1)
                reached(dve, y_step, b, 3, 2)
                reached(dve, tr_ok, b, HALF)
                dve.scalar_tensor_tensor(yz[:], tr[:], 1.0, yz[:], ALU.add, ALU.mult).then_inc(z_ok, 1)

            def scaled_product(a):
                reached(dve, ff_done, a)
                reached(dve, base1_ok, back(a, 2))
                for s in range(B):
                    i = dve.scalar_tensor_tensor(base0[a[1]][:, s, :], turn[:, s // 2, (s % 2) * C:(s % 2 + 1) * C],
                                                 lhs_scale[:, s:s + 1], rhs_scale[:], ALU.mult, ALU.mult)
                i.then_inc(ffn_ok, 1)

            def norm2(b):
                reached(dve, t2_done, b)
                x1 = xn[b[1]][:].rearrange("p b c -> p (b c)")
                dve.scalar_tensor_tensor(x1, turn[:].rearrange("p h w -> p (h w)"), 0.25, x1, ALU.mult,
                                         ALU.add).then_inc(x1_ok, 1)
                reached(dve, x1_ok, b)
                stats(xn[b[1]], st2, mv2, ln2_step, b, 3)
                dve.tensor_scalar(pw2[:], mv2[:, :, 1], EPS, None, ALU.add).then_inc(ln2_step, 1)

            def k_ramp(a):
                for h in range(HALF):
                    reached(dve, k_done, a, HALF, h)
                    dve.tensor_tensor(half(kt, h, 1, P + 1), seg(ring[:, (10 + h) % RING, :]),
                                      ramp[:, h, :].unsqueeze(1).broadcast_to([P, B, P]), ALU.subtract).then_inc(kt_ok, 1)

            def channel_mix(b):
                reached(dve, xb_ok, b, 2)
                reached(dve, xb_carry, b)
                dve.tensor_tensor(dxb[:], xb[b[1]][:, :, 1:P + 1], xb[b[1]][:, :, 0:P], ALU.subtract).then_inc(dxb_ok, 1)
                reached(dve, dxb_ok, b)
                for name, tile, done, per, ok in (("crr", xcr, rc_done, HALF, xcr_ok), ("crk", xck, h_done, HT, xck_ok)):
                    reached(dve, done, back(b, 1), per)
                    for h in range(HALF):
                        i = dve.scalar_tensor_tensor(seg(tile[:, h, :]), half(dxb, h), col(name, h), half(xb[b[1]], h),
                                                     ALU.mult, ALU.add)
                    i.then_inc(ok, 1)

            def step(t):
                a, b, c = t, back(t, 1), back(t, 2)
                if exists(a):
                    norm1_stats(a)
                if exists(b):
                    running_max(b)
                if exists(a):
                    norm1(a)
                if exists(b):
                    scan_s(b)
                if exists(a):
                    round_q(a)
                if exists(b):
                    log_ratio(b)
                if exists(a):
                    evac_q(a)
                    token_mix(a)
                if exists(b):
                    scan_aa(b)
                    gated(b)
                if exists(a):
                    scaled_product(a)
                if exists(b):
                    norm2(b)
                if exists(a):
                    k_ramp(a)
                if exists(b):
                    reached(dve, rsq2_ok, b)
                    dve.scalar_tensor_tensor(bias_2[:], mv2[:, :, 0], -1.0, rsq2[:], ALU.mult,
                                             ALU.mult).then_inc(bias2_ok, 1)
                if exists(c):
                    reached(dve, vc_step, c, HT)
                    reached(dve, tc_ok, c, HALF)
                    reached(dve, t4_done, back(c, 1))
                    dve.scalar_tensor_tensor(z2[:], tc[:], 1.0, vc[:], ALU.add, ALU.mult).then_inc(z2_ok, 1)
                if exists(b):
                    channel_mix(b)
                if exists(c):
                    reached(dve, t4_done, c)
                    reached(dve, base1_ok, c)
                    o = base1[c[1]][:].rearrange("p b c -> p (b c)")
                    dve.scalar_tensor_tensor(o, turn[:].rearrange("p h w -> p (h w)"), 0.5, o, ALU.mult,
                                             ALU.add).then_inc(out_ok, 1)

            iterations(dve, step)

        @block.tensor
        def _(pe):
            pe.wait_ge(ident_pool, 4)
            pe.wait_ge(rhs_in, 16)
            for h in range(HALF):
                for g in range(HALF):
                    i = pe.transpose(turn[:, h, g * P:(g + 1) * P], rhs_s[:, g, h * P:(h + 1) * P], ident[:])
            i.then_inc(setup_pe, 1)
            pe.wait_ge(setup_dve, 11)
            for h in range(HALF):
                pe.matmul(vc[:, 0, h * P:(h + 1) * P], ones[:], xn[0][:, h, 0:P], start=True, stop=True)
            for g in range(HALF):
                for h in range(HALF):
                    i = pe.transpose(turn[:, 0, :].bitcast(BF16)[:, g * C + h * P:g * C + (h + 1) * P],
                                     q_b[:, h, g * P:(g + 1) * P], ident_b[:])
            i.then_inc(setup_pe, 1)
            pe.wait_ge(setup_dve, 13)

            def project(bank, weights, act_tile, o):
                for g in range(HALF):
                    i = pe.matmul(ring[:, bank, :], weights[:, g, o * P:(o + 1) * P], act_tile[:, g, :],
                                  start=(g == 0), stop=(g == HALF - 1))
                return i

            def gate_c(c, t):
                reached(pe, xcr_ok, c)
                for h in range(HALF):
                    reached(pe, vs_ok, back(t, 1), HALF, h)
                    if known(t):
                        reached(pe, relu_ok, back(c, 1), HT, 6 + h)
                    project(h, wcr_s, xcr, h).then_inc(rc_done, 1)

            def hidden(c, j, t):
                if j == 0:
                    reached(pe, xck_ok, c)
                if j < 2:
                    reached(pe, tr_ok, back(t, 1), HALF, j)
                    if known(t):
                        reached(pe, relu_ok, back(c, 1), HT, 4 + j)
                elif j < 4:
                    reached(pe, tc_ok, c, HALF, j - 2)
                else:
                    reached(pe, relu_ok, c, HT, j - 4)
                project((2 + j) % RING, wck_s, xck, j).then_inc(h_done, 1)

            def value_c(c, j):
                reached(pe, kc_ok, c, HT, j)
                if j == 0:
                    reached(pe, z2_ok, back(c, 1))
                for h in range(HALF):
                    i = pe.matmul(vc[:, h, :], wcv_s[:, j, h * P:(h + 1) * P], kc[j % KC][:],
                                  start=(j == 0), stop=(j == HT - 1))
                i.then_inc(vc_step, 1)

            def turn_free(t):
                if known(t):
                    reached(pe, ffn_ok, back(t, 1))
                    reached(pe, xb_ok, back(t, 2), 2)
                    reached(pe, out_ok, back(t, 3))

            def to_channels(src, done, last=None):
                for h in range(HALF):
                    for s in range(B):
                        i = pe.transpose(turn[:, h, s * P:(s + 1) * P], src[:, s, h * P:(h + 1) * P], ident[:])
                i.then_inc(done, 1)

            def to_tokens(src, done):
                for s in range(B):
                    for h in range(HALF):
                        o = (s % 2) * C + h * P
                        i = pe.transpose(turn[:, s // 2, o:o + P], src[:, h, s * P:(s + 1) * P], ident[:])
                i.then_inc(done, 1)

            def turn_1(a):
                reached(pe, xz_ok, a)
                reached(pe, out_ok, back(a, 3))
                to_channels(nrm, t1_done)

            def turn_q(a):
                reached(pe, qb_ok, a)
                reached(pe, xa_ok, a, 2)
                for h in range(HALF):
                    for s in range(B):
                        o = h * W + s * P
                        i = pe.transpose(turn[:, 0, :].bitcast(BF16)[:, o:o + P], q_b[:, s, h * P:(h + 1) * P], ident_b[:])
                i.then_inc(tq_done, 1)

            def product_q(a):
                reached(pe, qc_ok, a)
                for s in range(B):
                    for h in range(HALF):
                        i = pe.matmul(turn[:, s // 2, (s % 2) * C:(s % 2 + 1) * C], q_c[:, h, s * P:(s + 1) * P],
                                      rhs_q[:, h, :], start=(h == 0), stop=(h == HALF - 1))
                i.then_inc(ff_done, 1)

            def kvr(a, first, tile, weights, ok, done, free, k0, per, t):
                reached(pe, ok, a)
                for h in range(HALF):
                    reached(pe, free[0], free[1], per, k0 + h)
                    if known(t):
                        reached(pe, (tr_ok if first == 10 else vs_ok), back(t, 1), HALF, h)
                    project((first + h) % RING, weights, tile, h).then_inc(done, 1)

            def step(t):
                a, b, c = t, back(t, 1), back(t, 2)
                turn_free(t)
                if exists(c):
                    if known(t):
                        pe.wait_ge(cm_in, 48)
                    gate_c(c, t)
                    hidden(c, 0, t)
                    hidden(c, 1, t)
                    value_c(c, 0)
                if exists(a):
                    turn_1(a)
                if exists(c):
                    hidden(c, 2, t)
                    value_c(c, 1)
                    hidden(c, 3, t)
                    value_c(c, 2)
                    hidden(c, 4, t)
                    value_c(c, 3)
                if exists(a):
                    turn_q(a)
                if exists(c):
                    hidden(c, 5, t)
                    value_c(c, 4)
                if exists(a):
                    product_q(a)
                if exists(c):
                    hidden(c, 6, t)
                    value_c(c, 5)
                    hidden(c, 7, t)
                    value_c(c, 6)
                    value_c(c, 7)
                if exists(b):
                    reached(pe, z_ok, b)
                    reached(pe, ffn_ok, a)
                    to_tokens(yz, t2_done)
                if exists(a):
                    if known(t):
                        pe.wait_ge(kvr_in, 48)
                    kvr(a, 10, xk, wk_s, xk_ok, k_done, (relu_ok, c), 4, HT, t)
                    kvr(a, 12, xv, wv_s, xv_ok, v_done, (relu_ok, c), 6, HT, t)
                if exists(b):
                    reached(pe, xbt_ok, b)
                    reached(pe, x1_ok, b)
                    to_channels(nrm, t3_done)
                if exists(a):
                    kvr(a, 14, xr, wr_s, xr_ok, r_done, (kt_ok, a), 0, HALF, t)
                if exists(c):
                    reached(pe, z2_ok, c)
                    reached(pe, xb_ok, b, 2)
                    to_tokens(z2, t4_done)

            iterations(pe, step)


def kernel(**inputs):
    import numpy as np
    import concourse.bacc as bacc
    from concourse.bass_utils import run_bass_kernel_spmd

    def get(name):
        return np.asarray(inputs["L0_" + name])

    vectors = {"g1": "attn_ln1_g", "b1": "attn_ln1_b", "rk": "attn_rk", "rv": "attn_rv", "rr": "attn_rr",
               "g2": "attn_ln2_g", "b2": "attn_ln2_b", "crk": "attn_crk", "crr": "attn_crr",
               "w": "attn_w", "u": "attn_u"}
    packed = np.stack([get(vectors[n]).reshape(HALF, P) for n in COLS])
    arrays = {
        "x": get("attn_x"),
        "cols": packed.transpose(2, 0, 1).reshape(P, len(COLS) * HALF),
        "wk": get("attn_Wk").T, "wv": get("attn_Wv").T, "wr": get("attn_Wr").T,
        "wcr": get("attn_Wcr").T, "wck": get("attn_Wck").T, "wcv": get("attn_Wcv").T,
        "rhs": get("ffn_rhs"),
    }
    arrays = {f"in_{n}": np.ascontiguousarray(a) for n, a in arrays.items()}
    nc = bacc.Bacc("TRN2", target_bir_lowering=False, num_devices=1)
    args = [nc.dram_tensor(n, a.shape, mybir.dt.from_np(a.dtype), kind="ExternalInput").ap() for n, a in arrays.items()]
    args.append(nc.dram_tensor("out", (B, T, C), F32, kind="ExternalOutput").ap())
    rwkv_program(nc, *args)
    r = run_bass_kernel_spmd(nc, [arrays], core_ids=[0])
    return r.results[0]["out"]
```

```python
from contextlib import ExitStack

import concourse.bass as bass
from concourse import mybir

P = 128
B, T, C, H = 4, 2048, 256, 1024
N = T // P
HALF = C // P
HT = H // P
SEG = HALF * B
W = B * P
RING = 4
KC = 4

F32 = mybir.dt.float32
BF16 = mybir.dt.bfloat16
I32 = mybir.dt.int32
F32R = mybir.dt.float32r
ALU = mybir.AluOpType
ACT = mybir.ActivationFunctionType
AX = mybir.AxisListType

EPS = 1e-5
NEG_INF = -1e38
BIG = 3e38
INT8_MAX = 127.0
MAGIC = 1.5 * 2.0**23

COLS = ["g1", "b1", "rk", "rv", "rr", "g2", "b2", "crk", "crr", "w", "u"]


def rwkv_program(nc, x, cols, wk, wv, wr, wcr, wck, wcv, rhs, out):
    ctx = ExitStack()
    with ctx:
        def sb(name, shape, dt=F32):
            return ctx.enter_context(nc.sbuf_tensor(name, shape, dt))

        def psum(name, shape, dt=F32):
            return ctx.enter_context(nc.psum_tensor(name, shape, dt))

        def sem(name):
            return ctx.enter_context(nc.semaphore(name))

        wk_s, wv_s, wr_s, wcr_s = (sb(n, [P, HALF, C]) for n in ("wk_s", "wv_s", "wr_s", "wcr_s"))
        wck_h, wck_l = sb("wck_h", [P, HALF, H], F32R), sb("wck_l", [P, HALF, H], F32R)
        wcv_s = sb("wcv_s", [P, HT, C])
        rhs_s = sb("rhs_s", [P, HALF, C])
        cols_s = sb("cols_s", [P, len(COLS), HALF])
        ident = sb("ident", [P, P])
        ident_b = sb("ident_b", [P, P], BF16)
        ones = sb("ones", [P, P])
        steps_i = sb("steps_i", [P, P], I32)
        steps_f = sb("steps_f", [P, P])
        ramp = sb("ramp", [P, HALF, P])
        ramp_end = sb("ramp_end", [P, SEG, 1])
        half_u = sb("half_u", [P, HALF])
        keep = sb("keep", [P, SEG, P + 1], BF16)
        zeros = sb("zeros", [P, SEG, 1])
        count = sb("count", [P, 2])
        neg_half = sb("neg_half", [P, 8])
        rhs_q = sb("rhs_q", [P, HALF, C], BF16)
        rhs_scale = sb("rhs_scale", [P, C])
        rq_amax = sb("rq_amax", [P, HALF])
        rq_scale = sb("rq_scale", [P, HALF])
        rq_inv = sb("rq_inv", [P, HALF])

        x_t = [sb(f"x_t{i}", [P, B, C]) for i in range(2)]
        xn = [sb(f"xn{i}", [P, B, C]) for i in range(2)]
        x1 = sb("x1", [P, B, C])
        nrm = sb("nrm", [P, B, C])
        q_f = sb("q_f", [P, B, C])
        q_b = sb("q_b", [P, B, C], BF16)
        base0 = [sb(f"base0_{i}", [P, B, C]) for i in range(2)]
        base1 = [sb(f"base1_{i}", [P, B, C]) for i in range(2)]
        st1, st2 = sb("st1", [P, B, 6]), sb("st2", [P, B, 6])
        mv1, mv2 = sb("mv1", [P, B, 2]), sb("mv2", [P, B, 2])
        pw1, rsq1 = sb("pw1", [P, 8]), sb("rsq1", [P, 8])
        rcp1 = sb("rcp1", [P, B])
        pw2, rsq2 = sb("pw2", [P, B]), sb("rsq2", [P, B])
        scale_z, bias_z = sb("scale_z", [P, B]), sb("bias_z", [P, B])
        bias_2 = sb("bias_2", [P, B])
        amax, lhs_inv = sb("amax", [P, B]), sb("lhs_inv", [P, B])
        lhs_scale = [sb(f"lhs_scale{i}", [P, B]) for i in range(2)]

        q_c = sb("q_c", [P, HALF, W], BF16)
        xa = [sb(f"xa{i}", [P, SEG, P + 1]) for i in range(2)]
        xb = [sb(f"xb{i}", [P, SEG, P + 1]) for i in range(2)]
        dx = sb("dx", [P, SEG, P])
        dxb = sb("dxb", [P, SEG, P])
        xk, xv, xr = (sb(n, [P, HALF, W]) for n in ("xk", "xv", "xr"))
        xck, xcr = sb("xck", [P, HALF, W]), sb("xcr", [P, HALF, W])
        kt = sb("kt", [P, SEG, P + 1])
        mx = sb("mx", [P, SEG, P + 1])
        dd = sb("dd", [P, SEG, P])
        decay = sb("decay", [P, SEG, P + 1])
        inject = sb("inject", [P, SEG, P + 1])
        ss = sb("ss", [P, SEG, P + 1])
        aa = sb("aa", [P, SEG, P + 1])
        tg = sb("tg", [P, SEG, P])
        vs = sb("vs", [P, HALF, W])
        tr = sb("tr", [P, HALF, W])
        yz = sb("yz", [P, HALF, W])
        tc = sb("tc", [P, HALF, W])
        z2 = sb("z2", [P, HALF, W])
        xck_h, xck_l = sb("xck_h", [P, HALF, W], F32R), sb("xck_l", [P, HALF, W], F32R)
        relu_h = [sb(f"relu_h{i}", [P, W]) for i in range(2)]
        kc = [sb(f"kc{i}", [P, W]) for i in range(KC)]

        ring = psum("ring", [P, RING, W])
        turn = psum("turn", [P, HALF, W])
        vc = psum("vc", [P, HALF, W])

        x_in = [sem("x_in0"), sem("x_in1")]
        stored = [sem("stored0"), sem("stored1")]
        cols_in, rhs_in = sem("cols_in"), sem("rhs_in")
        kvr_in, cm_in = sem("kvr_in"), sem("cm_in")
        consts_pool, ident_pool, setup_dve, setup_pe = sem("consts_pool"), sem("ident_pool"), sem("setup_dve"), sem("setup_pe")
        ln1_step, ln2_step = sem("ln1_step"), sem("ln2_step")
        rsq1_ok, rsq2_ok = sem("rsq1_ok"), sem("rsq2_ok")
        xz_scales, xz_ok, xn_ok, quant_scales = sem("xz_scales"), sem("xz_ok"), sem("xn_ok"), sem("quant_scales")
        qf_ok, qb_ok, qc_ok, ffn_ok, base0_ok = sem("qf_ok"), sem("qb_ok"), sem("qc_ok"), sem("ffn_ok"), sem("base0_ok")
        t1_done, tq_done, ff_done = sem("t1_done"), sem("tq_done"), sem("ff_done")
        t2_done, t3_done, t4_done = sem("t2_done"), sem("t3_done"), sem("t4_done")
        xa_ok, xa_carry, dx_ok, xk_ok, xv_ok, xr_ok = (sem(n) for n in ("xa_ok", "xa_carry", "dx_ok", "xk_ok", "xv_ok", "xr_ok"))
        k_done, v_done, r_done = sem("k_done"), sem("v_done"), sem("r_done")
        kt_ok, kt_carry, vs_ok, tr_ok = sem("kt_ok"), sem("kt_carry"), sem("vs_ok"), sem("tr_ok")
        mx_ok, d0_ok, relu_d, em_ok, ek_ok = sem("mx_ok"), sem("d0_ok"), sem("relu_d"), sem("em_ok"), sem("ek_ok")
        s_carry, ss_ok, ln_ok, d_ok = sem("s_carry"), sem("ss_ok"), sem("ln_ok"), sem("d_ok")
        relu_e, e1_ok, e2_ok, tg_ok = sem("relu_e"), sem("e1_ok"), sem("e2_ok"), sem("tg_ok")
        aa_carry, ev_ok, aa_ok, y_step, z_ok = sem("aa_carry"), sem("ev_ok"), sem("aa_ok"), sem("y_step"), sem("z_ok")
        x1_ok, bias2_ok, xbt_ok, xb_ok, xb_carry, dxb_ok = (sem(n) for n in ("x1_ok", "bias2_ok", "xbt_ok", "xb_ok", "xb_carry", "dxb_ok"))
        xck_hi, xck_lo, wck_split, wck_in = sem("xck_hi"), sem("xck_lo"), sem("wck_split"), sem("wck_in")
        xck_ok, xcr_ok, rc_done, tc_ok = sem("xck_ok"), sem("xcr_ok"), sem("rc_done"), sem("tc_ok")
        h_done, relu_ok, kc_ok, vc_step = sem("h_done"), sem("relu_ok"), sem("kc_ok"), sem("vc_step")
        z2_ok, base1_ok, out_ok = sem("z2_ok"), sem("base1_ok"), sem("out_ok")

        def back(t, k):
            d = t[1] - k
            return t[0] + d // 2, d % 2

        def known(c):
            return isinstance(c[0], int)

        def exists(c):
            return not known(c) or 0 <= 2 * c[0] + c[1] < N

        def reached(eng, s, c, per=1, k=None):
            k = per - 1 if k is None else k
            n = 2 * c[0] + c[1]
            if known(c):
                if n < 0:
                    return
                n = min(n, N - 1)
            eng.wait_ge(s, n * per + k + 1)

        def reached_dma(eng, sems, c):
            if known(c) and c[0] < 0:
                return
            eng.wait_ge(sems[c[1]], (c[0] + 1) * 16)

        def iterations(eng, step):
            for t in range(-1, 4):
                step((t // 2, t % 2))
            with eng.Fori(2, N // 2 - 1) as m:
                step((m, 0))
                step((m, 1))
            for t in range(N - 2, N + 2):
                step((t // 2, t % 2))

        def col(name, h):
            i = COLS.index(name)
            return cols_s[:, i, h:h + 1]

        def half(tile, h, a=0, b=P):
            return tile[:, B * h:B * (h + 1), a:b]

        def seg(ap):
            return ap.rearrange("p (b j) -> p b j", b=B)

        x_d = x.rearrange("b (n p) c -> n p b c", p=P)
        out_d = out.rearrange("b (n p) c -> n p b c", p=P)

        block = ctx.enter_context(nc.Block())

        @block.sync
        def _(sp):
            def load(c):
                sp.dma_start(x_t[c[1]][:], x_d[2 * c[0] + c[1]]).then_inc(x_in[c[1]], 16)

            load((0, 0))
            sp.dma_start(cols_s[:], cols.rearrange("p (i h) -> p i h", h=HALF)).then_inc(cols_in, 16)
            load((0, 1))
            for w_d, w_s in ((wk, wk_s), (wv, wv_s), (wr, wr_s)):
                sp.dma_start(w_s[:], w_d.rearrange("(h p) d -> p h d", p=P)).then_inc(kvr_in, 16)

            def step(t):
                ahead = back(t, -2)
                if exists(ahead) and exists(t):
                    reached(sp, base0_ok, t)
                    load(ahead)
                c = back(t, 2)
                if exists(c):
                    reached(sp, out_ok, c)
                    sp.dma_start(out_d[2 * c[0] + c[1]], base1[c[1]][:]).then_inc(stored[c[1]], 16)

            iterations(sp, step)
            sp.wait_ge(stored[0], 16 * (N // 2))
            sp.wait_ge(stored[1], 16 * (N // 2))

        @block.gpsimd
        def _(pool):
            pool.memset(ones[:], 1.0).then_inc(ident_pool, 1)
            pool.memset(neg_half[:], -0.5).then_inc(ident_pool, 1)
            pool.wait_ge(ident_pool, 2)
            pool.affine_select(out=ident[:], in_=ones[:], compare_op=ALU.is_equal, fill=0.0, base=0,
                               pattern=[[-1, P]], channel_multiplier=1).then_inc(ident_pool, 1)
            pool.iota(steps_i[:], pattern=[[1, P]], base=0, channel_multiplier=0).then_inc(ident_pool, 1)
            pool.memset(xa[1][:, :, P:P + 1], 0.0).then_inc(consts_pool, 1)
            pool.memset(xb[1][:, :, P:P + 1], 0.0).then_inc(consts_pool, 1)
            pool.memset(mx[:, :, P:P + 1], NEG_INF).then_inc(consts_pool, 1)
            pool.memset(ss[:, :, P:P + 1], 1.0).then_inc(consts_pool, 1)
            pool.memset(aa[:, :, P:P + 1], 0.0).then_inc(consts_pool, 1)
            pool.memset(decay[:, :, 0:1], 0.0).then_inc(consts_pool, 1)
            pool.memset(keep[:, :, 1:P + 1], BIG).then_inc(consts_pool, 1)
            pool.memset(keep[:, :, 0:1], -BIG).then_inc(consts_pool, 1)
            pool.memset(zeros[:], 0.0).then_inc(consts_pool, 1)
            pool.wait_ge(consts_pool, 9)
            pool.wait_ge(wck_split, 2 * HALF)

            def carry_xa(a):
                reached(pool, xr_ok, back(a, 2))
                reached(pool, xa_ok, back(a, 1), 2)
                pool.tensor_tensor(xa[a[1]][:, :, 0:1], xa[1 - a[1]][:, :, P:P + 1], zeros[:], ALU.add).then_inc(xa_carry, 1)

            def shift_difference(a):
                reached(pool, xa_ok, a, 2)
                reached(pool, xa_carry, a)
                reached(pool, xr_ok, back(a, 1))
                pool.tensor_tensor(dx[:], xa[a[1]][:, :, 1:P + 1], xa[a[1]][:, :, 0:P], ALU.subtract).then_inc(dx_ok, 1)

            def add_x(a):
                reached(pool, ffn_ok, a)
                reached_dma(pool, x_in, a)
                pool.tensor_tensor(base0[a[1]][:], base0[a[1]][:], x_t[a[1]][:], ALU.add).then_inc(base0_ok, 1)

            def carry_xb(b):
                reached(pool, xck_ok, back(b, 2))
                reached(pool, xb_ok, back(b, 1), 2)
                pool.tensor_tensor(xb[b[1]][:, :, 0:1], xb[1 - b[1]][:, :, P:P + 1], zeros[:], ALU.add).then_inc(xb_carry, 1)

            def root_2(b):
                reached(pool, ln2_step, b, 3)
                pool.tensor_tensor(rsq2[:], pw2[:], neg_half[:, 0:B], ALU.pow).then_inc(rsq2_ok, 1)

            def add_x1(b):
                reached(pool, base0_ok, b)
                reached(pool, x1_ok, b)
                reached_dma(pool, stored, back(b, 2))
                pool.tensor_tensor(base1[b[1]][:], base0[b[1]][:], x1[:], ALU.add).then_inc(base1_ok, 1)

            def root_1(n):
                reached(pool, ln1_step, n, 6)
                pool.tensor_tensor(rsq1[:], pw1[:], neg_half[:], ALU.pow).then_inc(rsq1_ok, 1)

            def step(t):
                nxt, a, b = back(t, -1), t, back(t, 1)
                if exists(a):
                    carry_xa(a)
                if exists(b):
                    carry_xb(b)
                if exists(a):
                    shift_difference(a)
                if exists(b):
                    root_2(b)
                if exists(nxt):
                    root_1(nxt)
                if exists(b):
                    add_x1(b)
                if exists(a):
                    add_x(a)

            iterations(pool, step)

        @block.scalar
        def _(act):
            act.dma_start(rhs_s[:], rhs.rearrange("(h p) d -> p h d", p=P)).then_inc(rhs_in, 16)
            for g in range(HALF):
                act.dma_start(base1[g][:].rearrange("p b c -> p (b c)"), wck[g * P:(g + 1) * P, :]).then_inc(wck_in, 16)
            for w_d, w_s in ((wcr, wcr_s), (wcv, wcv_s)):
                act.dma_start(w_s[:], w_d.rearrange("(h p) d -> p h d", p=P)).then_inc(cm_in, 16)
            act.wait_ge(setup_dve, 8)
            act.wait_ge(consts_pool, 9)

            def gate_c(c, h):
                reached(act, rc_done, c, HALF, h)
                if h == 0:
                    reached(act, z2_ok, back(c, 1))
                act.activation(tc[:, h, :], ring[:, h, :], ACT.Tanh, scale=0.5).then_inc(tc_ok, 1)

            def hidden(c, j):
                reached(act, h_done, c, HT, j)
                reached(act, kc_ok, c if j >= 2 else back(c, 1), HT, (j - 2) % HT)
                act.activation(relu_h[j % 2][:], ring[:, (2 + j) % RING, :], ACT.Relu).then_inc(relu_ok, 1)
                reached(act, relu_ok, c, HT, j)
                reached(act, vc_step, c if j >= KC else back(c, 1), HT, (j - KC) % HT)
                act.activation(kc[j % KC][:], relu_h[j % 2][:], ACT.Square).then_inc(kc_ok, 1)

            def norm_z(a):
                reached(act, xz_scales, a, 2)
                reached(act, t3_done, back(a, 2))
                reached(act, t1_done, back(a, 1))
                for b in range(B):
                    i = act.activation(nrm[:, b, :], x_t[a[1]][:, b, :], ACT.Identity,
                                       scale=scale_z[:, b:b + 1], bias=bias_z[:, b:b + 1])
                i.then_inc(xz_ok, 1)

            def falls(c, ready, relus):
                reached(act, ready, c)
                act.activation(decay[:, :, 1:P + 1], dd[:], ACT.Relu).then_inc(relus, 1)
                act.activation(inject[:, :, 1:P + 1], dd[:], ACT.Relu, scale=-1.0).then_inc(relus, 1)

            def exps(c, relus, low_ok, high_ok):
                reached(act, relus, c, 2, 0)
                act.activation(decay[:, :, 1:P + 1], decay[:, :, 1:P + 1], ACT.Exp, scale=-1.0).then_inc(low_ok, 1)
                reached(act, relus, c, 2, 1)
                act.activation(inject[:, :, 1:P + 1], inject[:, :, 1:P + 1], ACT.Exp, scale=-1.0).then_inc(high_ok, 1)

            def quant(a):
                reached(act, quant_scales, a, 3)
                reached(act, qb_ok, back(a, 1))
                for b in range(B):
                    i = act.activation(q_f[:, b, :], xn[a[1]][:, b, :], ACT.Copy, scale=lhs_inv[:, b:b + 1], bias=MAGIC)
                i.then_inc(qf_ok, 1)

            def evac_xa(a):
                reached(act, t1_done, a)
                reached(act, xr_ok, back(a, 2))
                reached(act, xa_carry, back(a, 1))
                for h in range(HALF):
                    act.activation(half(xa[a[1]], h, 1, P + 1), seg(turn[:, h, :]), ACT.Identity,
                                   scale=col("g1", h), bias=col("b1", h)).then_inc(xa_ok, 1)

            def evac_xb(b):
                reached(act, t3_done, b)
                reached(act, xck_ok, back(b, 2))
                reached(act, xb_carry, back(b, 1))
                for h in range(HALF):
                    act.activation(half(xb[b[1]], h, 1, P + 1), seg(turn[:, h, :]), ACT.Identity,
                                   scale=col("g2", h), bias=col("b2", h)).then_inc(xb_ok, 1)

            def value(a, b, h):
                if h == 0:
                    reached(act, y_step, b, 3, 0)
                reached(act, v_done, a, HALF, h)
                act.activation(vs[:, h, :], ring[:, (12 + h) % RING, :], ACT.Copy).then_inc(vs_ok, 1)

            def gate_r(a, b, h):
                if h == 0:
                    reached(act, z_ok, b)
                reached(act, r_done, a, HALF, h)
                act.activation(tr[:, h, :], ring[:, (14 + h) % RING, :], ACT.Tanh, scale=0.5).then_inc(tr_ok, 1)

            def ln_s(b):
                reached(act, ss_ok, b)
                act.activation(kt[:, :, 0:P], ss[:, :, 0:P], ACT.Ln).then_inc(ln_ok, 1)

            def gate_u(b):
                reached(act, z_ok, back(b, 1))
                for h in range(HALF):
                    i = act.activation(half(tg, h), half(dd, h), ACT.Tanh, scale=0.5, bias=half_u[:, h:h + 1])
                i.then_inc(tg_ok, 1)

            def norm_x1(a, b):
                reached(act, bias2_ok, b)
                reached(act, t1_done, a)
                for s in range(B):
                    i = act.activation(nrm[:, s, :], x1[:, s, :], ACT.Identity,
                                       scale=rsq2[:, s:s + 1], bias=bias_2[:, s:s + 1])
                i.then_inc(xbt_ok, 1)

            def xck_high(b, c):
                reached(act, xck_ok, b)
                reached(act, h_done, c, HT)
                act.activation(xck_h[:], xck[:], ACT.Copy).then_inc(xck_hi, 1)

            def step(t):
                nxt, a, b, c = back(t, -1), t, back(t, 1), back(t, 2)
                if exists(c):
                    gate_c(c, 0)
                    gate_c(c, 1)
                if exists(b):
                    ln_s(b)
                if exists(c):
                    hidden(c, 0)
                    hidden(c, 1)
                if exists(b):
                    falls(b, d_ok, relu_e)
                    exps(b, relu_e, e1_ok, e2_ok)
                if exists(c):
                    hidden(c, 2)
                    hidden(c, 3)
                if exists(b):
                    gate_u(b)
                if exists(a):
                    evac_xa(a)
                if exists(c):
                    hidden(c, 4)
                    hidden(c, 5)
                    hidden(c, 6)
                    hidden(c, 7)
                if exists(b):
                    norm_x1(a, b)
                    evac_xb(b)
                if exists(nxt):
                    norm_z(nxt)
                if exists(a):
                    value(a, b, 0)
                    falls(a, d0_ok, relu_d)
                    exps(a, relu_d, em_ok, ek_ok)
                if exists(b):
                    xck_high(b, c)
                if exists(a):
                    gate_r(a, b, 0)
                    value(a, b, 1)
                    gate_r(a, b, 1)
                if exists(nxt):
                    quant(nxt)

            iterations(act, step)

        @block.vector
        def _(dve):
            dve.wait_ge(ident_pool, 4)
            dve.wait_ge(cols_in, 16)
            dve.tensor_copy(ident_b[:], ident[:]).then_inc(setup_dve, 1)
            dve.tensor_copy(steps_f[:], steps_i[:]).then_inc(setup_dve, 1)
            dve.wait_ge(setup_dve, 2)
            for h in range(HALF):
                dve.tensor_scalar(ramp[:, h, :], steps_f[:], col("w", h), None, ALU.mult)
                dve.tensor_scalar(ramp_end[:, B * h:B * (h + 1), :], ones[:, 0:B].unsqueeze(2), col("w", h), float(P),
                                  ALU.mult, ALU.mult).then_inc(setup_dve, 1)
            dve.tensor_scalar(half_u[:], cols_s[:, COLS.index("u"), :], 0.5, None, ALU.mult).then_inc(setup_dve, 1)
            dve.wait_ge(setup_pe, 1)
            dve.tensor_reduce(rq_amax[:], turn[:, :, 0:C], AX.X, ALU.max,
                              apply_absolute_value=True).then_inc(setup_dve, 1)
            dve.wait_ge(setup_dve, 6)
            dve.tensor_scalar(rq_scale[:], rq_amax[:], 1e-12, 1.0 / INT8_MAX, ALU.max, ALU.mult).then_inc(setup_dve, 1)
            dve.wait_ge(setup_dve, 7)
            dve.reciprocal(rq_inv[:], rq_scale[:]).then_inc(setup_dve, 1)
            dve.wait_ge(setup_dve, 8)
            for h in range(HALF):
                dve.tensor_scalar(q_f[:, h, :], turn[:, h, 0:C], rq_inv[:, h:h + 1], MAGIC, ALU.mult, ALU.add)
                dve.tensor_scalar(xn[0][:, h, 0:P], ident[:], rq_scale[:, h:h + 1], None, ALU.mult).then_inc(setup_dve, 1)
            dve.wait_ge(setup_dve, 10)
            dve.tensor_scalar(q_b[:, 0:HALF, :], q_f[:, 0:HALF, :], MAGIC + INT8_MAX, MAGIC,
                              ALU.min, ALU.subtract).then_inc(setup_dve, 1)
            dve.wait_ge(setup_pe, 2)
            dve.tensor_scalar(rhs_q[:], turn[:, 0, :].bitcast(BF16)[:, 0:HALF * C].rearrange("p (h d) -> p h d", h=HALF),
                              -INT8_MAX, None, ALU.max).then_inc(setup_dve, 1)
            dve.tensor_copy(rhs_scale[:], vc[:, 0, 0:C]).then_inc(setup_dve, 1)
            dve.wait_ge(consts_pool, 9)
            dve.wait_ge(setup_dve, 13)
            dve.wait_ge(wck_in, 16 * HALF)
            for g in range(HALF):
                dve.tensor_copy(wck_h[:, g, :], base1[g][:].rearrange("p b c -> p (b c)")).then_inc(wck_split, 1)
            dve.wait_ge(wck_split, HALF)
            for g in range(HALF):
                dve.tensor_tensor(wck_l[:, g, :], base1[g][:].rearrange("p b c -> p (b c)"), wck_h[:, g, :].bitcast(F32),
                                  ALU.subtract).then_inc(wck_split, 1)

            def stats(tile, st, mv, steps, c, per):
                for s in range(B):
                    i = dve.bn_stats(st[:, s, :], tile[:, s, :])
                i.then_inc(steps, 1)
                reached(dve, steps, c, per, 0)
                dve.tensor_copy(count[:, 0:1], st[:, 0, 0:1])
                for s in range(B):
                    i = dve.bn_aggr(mv[:, s, :], st[:, s, :])
                i.then_inc(steps, 1)
                reached(dve, steps, c, per, 1)

            def norm1_stats(a):
                reached_dma(dve, x_in, a)
                stats(x_t[a[1]], st1, mv1, ln1_step, a, 6)
                dve.tensor_scalar(pw1[:, 0:B], mv1[:, :, 1], EPS, None, ALU.add).then_inc(ln1_step, 1)
                reached(dve, ln1_step, a, 6, 2)
                dve.reciprocal(rcp1[:], pw1[:, 0:B]).then_inc(ln1_step, 1)
                reached(dve, ln1_step, a, 6, 3)
                dve.tensor_tensor(rcp1[:], mv1[:, :, 1], rcp1[:], ALU.mult).then_inc(ln1_step, 1)
                reached(dve, ln1_step, a, 6, 4)
                dve.tensor_scalar(pw1[:, B:2 * B], rcp1[:], EPS, None, ALU.add).then_inc(ln1_step, 1)

            def running_max(b):
                dve.tensor_tensor(kt[:, :, 0:1], mx[:, :, P:P + 1], ramp_end[:], ALU.add).then_inc(kt_carry, 1)
                reached(dve, kt_ok, b, HALF)
                reached(dve, kt_carry, b)
                dve.tensor_tensor_scan(mx[:].rearrange("p s j -> p (s j)"), keep[:].rearrange("p s j -> p (s j)"),
                                       kt[:].rearrange("p s j -> p (s j)"), 0.0, ALU.min, ALU.max).then_inc(mx_ok, 1)
                reached(dve, mx_ok, b)
                dve.tensor_tensor(dd[:], kt[:, :, 1:P + 1], mx[:, :, 0:P], ALU.subtract).then_inc(d0_ok, 1)

            def norm1(a):
                reached(dve, rsq1_ok, a)
                reached(dve, xz_ok, back(a, 1))
                dve.tensor_tensor(scale_z[:], rsq1[:, 0:B], rsq1[:, B:2 * B], ALU.mult).then_inc(xz_scales, 1)
                reached(dve, xz_scales, a, 2, 0)
                dve.scalar_tensor_tensor(bias_z[:], mv1[:, :, 0], -1.0, scale_z[:], ALU.mult,
                                         ALU.mult).then_inc(xz_scales, 1)

            def norm1_quant(a):
                reached(dve, qf_ok, back(a, 1))
                for s in range(B):
                    i = dve.tensor_scalar(xn[a[1]][:, s, :], x_t[a[1]][:, s, :], mv1[:, s, 0:1], rsq1[:, s:s + 1],
                                          ALU.subtract, ALU.mult)
                i.then_inc(xn_ok, 1)
                reached(dve, xn_ok, a)
                dve.tensor_reduce(amax[:], xn[a[1]][:], AX.X, ALU.max, apply_absolute_value=True).then_inc(quant_scales, 1)
                reached(dve, quant_scales, a, 3, 0)
                dve.tensor_scalar(lhs_scale[a[1]][:], amax[:], 1e-12, 1.0 / INT8_MAX, ALU.max, ALU.mult).then_inc(quant_scales, 1)
                reached(dve, quant_scales, a, 3, 1)
                dve.reciprocal(lhs_inv[:], lhs_scale[a[1]][:]).then_inc(quant_scales, 1)

            def scan_s(b):
                reached(dve, em_ok, b)
                reached(dve, ek_ok, b)
                dve.tensor_copy(inject[:, :, 0:1], ss[:, :, P:P + 1]).then_inc(s_carry, 1)
                reached(dve, s_carry, b)
                dve.tensor_tensor_scan(ss[:].rearrange("p s j -> p (s j)"), decay[:].rearrange("p s j -> p (s j)"),
                                       inject[:].rearrange("p s j -> p (s j)"), 0.0, ALU.mult, ALU.add).then_inc(ss_ok, 1)

            def round_q(a):
                reached(dve, qf_ok, a)
                reached(dve, tq_done, back(a, 1))
                dve.tensor_scalar(q_b[:], q_f[:], MAGIC + INT8_MAX, MAGIC, ALU.min, ALU.subtract).then_inc(qb_ok, 1)

            def log_ratio(b):
                reached(dve, ln_ok, b)
                dve.tensor_tensor(dd[:], dd[:], kt[:, :, 0:P], ALU.subtract).then_inc(d_ok, 1)

            def evac_q(a):
                reached(dve, tq_done, a)
                reached(dve, ff_done, back(a, 1))
                dve.tensor_scalar(q_c[:], turn[:, 0, :].bitcast(BF16).rearrange("p (h w) -> p h w", h=HALF),
                                  -INT8_MAX, None, ALU.max).then_inc(qc_ok, 1)

            def token_mix(a, name, tile, done, ok):
                reached(dve, dx_ok, a)
                reached(dve, done, back(a, 1), HALF)
                for h in range(HALF):
                    i = dve.scalar_tensor_tensor(seg(tile[:, h, :]), half(dx, h), col(name, h), half(xa[a[1]], h),
                                                 ALU.mult, ALU.add)
                i.then_inc(ok, 1)

            def scan_aa(b):
                reached(dve, e2_ok, b)
                reached(dve, vs_ok, b, HALF)
                dve.tensor_copy(inject[:, :, 0:1], aa[:, :, P:P + 1]).then_inc(aa_carry, 1)
                dve.tensor_tensor(inject[:, :, 1:P + 1], inject[:, :, 1:P + 1],
                                  vs[:].rearrange("p h (b j) -> p (h b) j", b=B), ALU.mult).then_inc(ev_ok, 1)
                reached(dve, aa_carry, b)
                reached(dve, ev_ok, b)
                reached(dve, e1_ok, b)
                dve.tensor_tensor_scan(aa[:].rearrange("p s j -> p (s j)"), decay[:].rearrange("p s j -> p (s j)"),
                                       inject[:].rearrange("p s j -> p (s j)"), 0.0, ALU.mult, ALU.add).then_inc(aa_ok, 1)

            def value_step(b):
                y = yz[:].rearrange("p h (b j) -> p (h b) j", b=B)
                reached(dve, aa_ok, b)
                reached(dve, t2_done, back(b, 1))
                dve.tensor_tensor(y, vs[:].rearrange("p h (b j) -> p (h b) j", b=B), aa[:, :, 0:P],
                                  ALU.subtract).then_inc(y_step, 1)

            def gated(b):
                y = yz[:].rearrange("p h (b j) -> p (h b) j", b=B)
                reached(dve, y_step, b, 3, 0)
                reached(dve, tg_ok, b)
                dve.scalar_tensor_tensor(y, tg[:], 1.0, y, ALU.add, ALU.mult).then_inc(y_step, 1)
                reached(dve, y_step, b, 3, 1)
                dve.scalar_tensor_tensor(y, aa[:, :, 0:P], 2.0, y, ALU.mult, ALU.add).then_inc(y_step, 1)
                reached(dve, y_step, b, 3, 2)
                reached(dve, tr_ok, b, HALF)
                dve.scalar_tensor_tensor(yz[:], tr[:], 1.0, yz[:], ALU.add, ALU.mult).then_inc(z_ok, 1)

            def scaled_product(a):
                reached(dve, ff_done, a)
                reached(dve, base1_ok, back(a, 2))
                for s in range(B):
                    i = dve.scalar_tensor_tensor(base0[a[1]][:, s, :], turn[:, s // 2, (s % 2) * C:(s % 2 + 1) * C],
                                                 lhs_scale[a[1]][:, s:s + 1], rhs_scale[:], ALU.mult, ALU.mult)
                i.then_inc(ffn_ok, 1)

            def norm2(b):
                reached(dve, t2_done, b)
                reached(dve, base1_ok, back(b, 1))
                reached(dve, xbt_ok, back(b, 1))
                dve.scalar_tensor_tensor(x1[:].rearrange("p b c -> p (b c)"), turn[:].rearrange("p h w -> p (h w)"), 0.25,
                                         xn[b[1]][:].rearrange("p b c -> p (b c)"), ALU.mult, ALU.add).then_inc(x1_ok, 1)
                reached(dve, x1_ok, b)
                stats(x1, st2, mv2, ln2_step, b, 3)
                dve.tensor_scalar(pw2[:], mv2[:, :, 1], EPS, None, ALU.add).then_inc(ln2_step, 1)

            def k_ramp(a, h):
                reached(dve, k_done, a, HALF, h)
                dve.tensor_tensor(half(kt, h, 1, P + 1), seg(ring[:, (10 + h) % RING, :]),
                                  ramp[:, h, :].unsqueeze(1).broadcast_to([P, B, P]), ALU.subtract).then_inc(kt_ok, 1)

            def mix_to(b, name, tile, done, per, ok):
                reached(dve, done, back(b, 1), per)
                for h in range(HALF):
                    i = dve.scalar_tensor_tensor(seg(tile[:, h, :]), half(dxb, h), col(name, h), half(xb[b[1]], h),
                                                 ALU.mult, ALU.add)
                i.then_inc(ok, 1)

            def receptance_mix(b):
                reached(dve, xb_ok, b, 2)
                reached(dve, xb_carry, b)
                dve.tensor_tensor(dxb[:], xb[b[1]][:, :, 1:P + 1], xb[b[1]][:, :, 0:P], ALU.subtract).then_inc(dxb_ok, 1)
                reached(dve, dxb_ok, b)
                mix_to(b, "crr", xcr, rc_done, HALF, xcr_ok)

            def key_mix(b):
                mix_to(b, "crk", xck, h_done, HT, xck_ok)

            def xck_low(b):
                reached(dve, xck_hi, b)
                dve.tensor_tensor(xck_l[:], xck[:], xck_h[:].bitcast(F32), ALU.subtract).then_inc(xck_lo, 1)

            def value_gated(c):
                reached(dve, vc_step, c, HT)
                reached(dve, tc_ok, c, HALF)
                reached(dve, t4_done, back(c, 1))
                dve.scalar_tensor_tensor(z2[:], tc[:], 1.0, vc[:], ALU.add, ALU.mult).then_inc(z2_ok, 1)

            def result(c):
                reached(dve, t4_done, c)
                reached(dve, base1_ok, c)
                o = base1[c[1]][:].rearrange("p b c -> p (b c)")
                dve.scalar_tensor_tensor(o, turn[:].rearrange("p h w -> p (h w)"), 0.5, o, ALU.mult,
                                         ALU.add).then_inc(out_ok, 1)

            def bias2(b):
                reached(dve, rsq2_ok, b)
                dve.scalar_tensor_tensor(bias_2[:], mv2[:, :, 0], -1.0, rsq2[:], ALU.mult,
                                         ALU.mult).then_inc(bias2_ok, 1)

            def step(t):
                nxt, a, b, c = back(t, -1), t, back(t, 1), back(t, 2)
                if exists(b):
                    scan_s(b)
                if exists(a):
                    round_q(a)
                    evac_q(a)
                if exists(b):
                    log_ratio(b)
                if exists(nxt):
                    norm1_stats(nxt)
                if exists(b):
                    scan_aa(b)
                    value_step(b)
                    gated(b)
                if exists(a):
                    scaled_product(a)
                    token_mix(a, "rk", xk, k_done, xk_ok)
                if exists(b):
                    norm2(b)
                if exists(a):
                    token_mix(a, "rv", xv, v_done, xv_ok)
                if exists(b):
                    bias2(b)
                if exists(a):
                    token_mix(a, "rr", xr, r_done, xr_ok)
                if exists(nxt):
                    norm1(nxt)
                if exists(a):
                    k_ramp(a, 0)
                    k_ramp(a, 1)
                    running_max(a)
                if exists(b):
                    receptance_mix(b)
                if exists(c):
                    value_gated(c)
                if exists(b):
                    key_mix(b)
                if exists(nxt):
                    norm1_quant(nxt)
                if exists(c):
                    result(c)
                if exists(b):
                    xck_low(b)

            iterations(dve, step)

        @block.tensor
        def _(pe):
            pe.wait_ge(ident_pool, 4)
            pe.wait_ge(rhs_in, 16)
            for h in range(HALF):
                for g in range(HALF):
                    i = pe.transpose(turn[:, h, g * P:(g + 1) * P], rhs_s[:, g, h * P:(h + 1) * P], ident[:])
            i.then_inc(setup_pe, 1)
            pe.wait_ge(setup_dve, 11)
            for h in range(HALF):
                pe.matmul(vc[:, 0, h * P:(h + 1) * P], ones[:], xn[0][:, h, 0:P], start=True, stop=True)
            for g in range(HALF):
                for h in range(HALF):
                    i = pe.transpose(turn[:, 0, :].bitcast(BF16)[:, g * C + h * P:g * C + (h + 1) * P],
                                     q_b[:, h, g * P:(g + 1) * P], ident_b[:])
            i.then_inc(setup_pe, 1)
            pe.wait_ge(setup_dve, 13)

            def project(bank, weights, act_tile, o):
                for g in range(HALF):
                    i = pe.matmul(ring[:, bank, :], weights[:, g, o * P:(o + 1) * P], act_tile[:, g, :],
                                  start=(g == 0), stop=(g == HALF - 1))
                return i

            def project3(bank, weights, act_tile, o):
                terms = [(w, x, g) for w, x in ((0, 0), (1, 0), (0, 1)) for g in range(HALF)]
                for n, (w, x, g) in enumerate(terms):
                    i = pe.matmul(ring[:, bank, :], weights[w][:, g, o * P:(o + 1) * P], act_tile[x][:, g, :],
                                  start=(n == 0), stop=(n == len(terms) - 1))
                return i

            def gate_c(c, t, h):
                if h == 0:
                    reached(pe, xcr_ok, c)
                reached(pe, vs_ok, back(t, 1), HALF, h)
                if known(t):
                    reached(pe, relu_ok, back(c, 1), HT, 6 + h)
                project(h, wcr_s, xcr, h).then_inc(rc_done, 1)

            def hidden(c, j, t):
                if j == 0:
                    reached(pe, xck_lo, c)
                if j < 2:
                    reached(pe, tr_ok, back(t, 1), HALF, j)
                    if known(t):
                        reached(pe, relu_ok, back(c, 1), HT, 4 + j)
                elif j < 4:
                    reached(pe, tc_ok, c, HALF, j - 2)
                else:
                    reached(pe, relu_ok, c, HT, j - 4)
                project3((2 + j) % RING, (wck_h, wck_l), (xck_h, xck_l), j).then_inc(h_done, 1)

            def value_c(c, j):
                reached(pe, kc_ok, c, HT, j)
                if j == 0:
                    reached(pe, z2_ok, back(c, 1))
                for h in range(HALF):
                    i = pe.matmul(vc[:, h, :], wcv_s[:, j, h * P:(h + 1) * P], kc[j % KC][:],
                                  start=(j == 0), stop=(j == HT - 1))
                i.then_inc(vc_step, 1)

            def turn_free(t):
                if known(t):
                    reached(pe, ffn_ok, back(t, 1))
                    reached(pe, xb_ok, back(t, 2), 2)
                    reached(pe, out_ok, back(t, 3))

            def to_channels(src, done, last=None):
                for h in range(HALF):
                    for s in range(B):
                        i = pe.transpose(turn[:, h, s * P:(s + 1) * P], src[:, s, h * P:(h + 1) * P], ident[:])
                i.then_inc(done, 1)

            def to_tokens(src, done):
                for s in range(B):
                    for h in range(HALF):
                        o = (s % 2) * C + h * P
                        i = pe.transpose(turn[:, s // 2, o:o + P], src[:, h, s * P:(s + 1) * P], ident[:])
                i.then_inc(done, 1)

            def turn_1(a):
                reached(pe, xz_ok, a)
                reached(pe, qc_ok, a)
                to_channels(nrm, t1_done)

            def turn_q(a):
                reached(pe, qb_ok, a)
                reached(pe, out_ok, back(a, 3))
                for h in range(HALF):
                    for s in range(B):
                        o = h * W + s * P
                        i = pe.transpose(turn[:, 0, :].bitcast(BF16)[:, o:o + P], q_b[:, s, h * P:(h + 1) * P], ident_b[:])
                i.then_inc(tq_done, 1)

            def product_q(a):
                reached(pe, xa_ok, a, 2)
                for s in range(B):
                    for h in range(HALF):
                        i = pe.matmul(turn[:, s // 2, (s % 2) * C:(s % 2 + 1) * C], q_c[:, h, s * P:(s + 1) * P],
                                      rhs_q[:, h, :], start=(h == 0), stop=(h == HALF - 1))
                i.then_inc(ff_done, 1)

            def key(a, c, h):
                reached(pe, xk_ok, a)
                reached(pe, relu_ok, c, HT, 4 + h)
                if known(a):
                    reached(pe, tr_ok, back(a, 1), HALF, h)
                project((10 + h) % RING, wk_s, xk, h).then_inc(k_done, 1)

            def value(a, c, h):
                reached(pe, xv_ok, a)
                reached(pe, relu_ok, c, HT, 6 + h)
                if known(a):
                    reached(pe, vs_ok, back(a, 1), HALF, h)
                project((12 + h) % RING, wv_s, xv, h).then_inc(v_done, 1)

            def receptance(a, h):
                reached(pe, xr_ok, a)
                reached(pe, kt_ok, a, HALF, h)
                project((14 + h) % RING, wr_s, xr, h).then_inc(r_done, 1)

            def turn_2(a, b):
                reached(pe, z_ok, b)
                reached(pe, ffn_ok, a)
                to_tokens(yz, t2_done)

            def turn_3(b):
                reached(pe, xbt_ok, b)
                reached(pe, x1_ok, b)
                to_channels(nrm, t3_done)

            def turn_4(b, c):
                reached(pe, z2_ok, c)
                reached(pe, xb_ok, b, 2)
                to_tokens(z2, t4_done)

            def step(t):
                a, b, c = t, back(t, 1), back(t, 2)
                turn_free(t)
                if known(t):
                    if exists(c):
                        pe.wait_ge(cm_in, 32)
                        pe.wait_ge(wck_split, 2 * HALF)
                    if exists(a):
                        pe.wait_ge(kvr_in, 48)
                if exists(c):
                    gate_c(c, t, 0)
                    gate_c(c, t, 1)
                    hidden(c, 0, t)
                    hidden(c, 1, t)
                if exists(a):
                    turn_q(a)
                if exists(c):
                    hidden(c, 2, t)
                    hidden(c, 3, t)
                    hidden(c, 4, t)
                if exists(a):
                    turn_1(a)
                if exists(c):
                    value_c(c, 0)
                    hidden(c, 5, t)
                    value_c(c, 1)
                    hidden(c, 6, t)
                    value_c(c, 2)
                if exists(a):
                    product_q(a)
                if exists(c):
                    value_c(c, 3)
                    value_c(c, 4)
                if exists(b):
                    turn_2(a, b)
                if exists(c):
                    hidden(c, 7, t)
                    value_c(c, 5)
                if exists(a):
                    key(a, c, 0)
                    key(a, c, 1)
                    value(a, c, 0)
                if exists(b):
                    turn_3(b)
                if exists(c):
                    value_c(c, 6)
                    value_c(c, 7)
                if exists(a):
                    value(a, c, 1)
                    receptance(a, 0)
                    receptance(a, 1)
                if exists(c):
                    turn_4(b, c)

            iterations(pe, step)


def kernel(**inputs):
    import numpy as np
    import concourse.bacc as bacc
    from concourse.bass_utils import run_bass_kernel_spmd

    def get(name):
        return np.asarray(inputs["L0_" + name])

    vectors = {"g1": "attn_ln1_g", "b1": "attn_ln1_b", "rk": "attn_rk", "rv": "attn_rv", "rr": "attn_rr",
               "g2": "attn_ln2_g", "b2": "attn_ln2_b", "crk": "attn_crk", "crr": "attn_crr",
               "w": "attn_w", "u": "attn_u"}
    packed = np.stack([get(vectors[n]).reshape(HALF, P) for n in COLS])
    arrays = {
        "x": get("attn_x"),
        "cols": packed.transpose(2, 0, 1).reshape(P, len(COLS) * HALF),
        "wk": get("attn_Wk").T, "wv": get("attn_Wv").T, "wr": get("attn_Wr").T,
        "wcr": get("attn_Wcr").T, "wck": get("attn_Wck").T, "wcv": get("attn_Wcv").T,
        "rhs": get("ffn_rhs"),
    }
    arrays = {f"in_{n}": np.ascontiguousarray(a) for n, a in arrays.items()}
    nc = bacc.Bacc("TRN2", target_bir_lowering=False, num_devices=1)
    args = [nc.dram_tensor(n, a.shape, mybir.dt.from_np(a.dtype), kind="ExternalInput").ap() for n, a in arrays.items()]
    args.append(nc.dram_tensor("out", (B, T, C), F32, kind="ExternalOutput").ap())
    rwkv_program(nc, *args)
    r = run_bass_kernel_spmd(nc, [arrays], core_ids=[0])
    return r.results[0]["out"]
```

```python
from contextlib import ExitStack

import concourse.bass as bass
from concourse import mybir

P = 128
B, T, C, H = 4, 2048, 256, 1024
N = T // P
HALF = C // P
HT = H // P
SEG = HALF * B
W = B * P
RING = 4
PAIRS = HT // 2
KC = 2

F32 = mybir.dt.float32
BF16 = mybir.dt.bfloat16
F32R = mybir.dt.float32r
ALU = mybir.AluOpType
ACT = mybir.ActivationFunctionType
AX = mybir.AxisListType

EPS = 1e-5
NEG_INF = -1e38
BIG = 2e38
INT8_MAX = 127.0
MAGIC = 1.5 * 2.0**23

COLS = ["g1", "b1", "rk", "rv", "rr", "g2", "b2", "crk", "crr", "w", "u"]


def rwkv_program(nc, x, cols, wk, wv, wr, wcr, wck, wcv, rhs, out):
    ctx = ExitStack()
    with ctx:
        def sb(name, shape, dt=F32):
            return ctx.enter_context(nc.sbuf_tensor(name, shape, dt))

        def psum(name, shape, dt=F32):
            return ctx.enter_context(nc.psum_tensor(name, shape, dt))

        def sem(name):
            return ctx.enter_context(nc.semaphore(name))

        wk_s, wv_s, wr_s, wcr_s = (sb(n, [P, HALF, C]) for n in ("wk_s", "wv_s", "wr_s", "wcr_s"))
        wck_h, wck_l = sb("wck_h", [P, HALF, H], F32R), sb("wck_l", [P, HALF, H], F32R)
        wcv_s = sb("wcv_s", [P, PAIRS, C])
        wcv_h, wcv_l = sb("wcv_h", [P, PAIRS, C], F32R), sb("wcv_l", [P, PAIRS, C], F32R)
        cols_s = sb("cols_s", [P, len(COLS) + 1, HALF])
        half_u = cols_s[:, len(COLS), :]
        ident = sb("ident", [P, P])
        ident_b = sb("ident_b", [P, P], BF16)
        rise = sb("rise", [P, SEG, P + 1])
        zeros = sb("zeros", [P, SEG, 1])
        count = sb("count", [P, 2])
        neg_half = sb("neg_half", [P, 8])
        rhs_q = sb("rhs_q", [P, HALF, C], BF16)
        rhs_scale = sb("rhs_scale", [P, C])

        x_t = [sb(f"x_t{i}", [P, B, C]) for i in range(2)]
        xn = [sb(f"xn{i}", [P, B, C]) for i in range(2)]
        x1 = sb("x1", [P, B, C])
        nrm = sb("nrm", [P, B, C])
        q_f = sb("q_f", [P, B, C])
        q_b = sb("q_b", [P, B, C], BF16)
        base0 = [sb(f"base0_{i}", [P, B, C]) for i in range(2)]
        base1 = [sb(f"base1_{i}", [P, B, C]) for i in range(2)]
        st1, st2 = sb("st1", [P, B, 6]), sb("st2", [P, B, 6])
        mv1, mv2 = sb("mv1", [P, B, 2]), sb("mv2", [P, B, 2])
        pw1, rsq1 = sb("pw1", [P, 8]), sb("rsq1", [P, 8])
        pw2, rsq2 = sb("pw2", [P, B]), sb("rsq2", [P, B])
        bias_z = sb("bias_z", [P, B])
        bias_2 = sb("bias_2", [P, B])
        amax, lhs_inv = sb("amax", [P, B]), sb("lhs_inv", [P, B])
        lhs_scale = [sb(f"lhs_scale{i}", [P, B]) for i in range(2)]

        q_c = sb("q_c", [P, HALF, W], BF16)
        xa = [sb(f"xa{i}", [P, SEG, P + 1]) for i in range(2)]
        xb = [sb(f"xb{i}", [P, SEG, P + 1]) for i in range(2)]
        dx = sb("dx", [P, SEG, P])
        dxb = sb("dxb", [P, SEG, P])
        xk, xv, xr = (sb(n, [P, HALF, W]) for n in ("xk", "xv", "xr"))
        xck, xcr = sb("xck", [P, HALF, W]), sb("xcr", [P, HALF, W])
        kt = sb("kt", [P, SEG, P + 1])
        mx = sb("mx", [P, SEG, P + 1])
        dd = sb("dd", [P, SEG, P])
        decay = sb("decay", [P, SEG, P + 1])
        inject = sb("inject", [P, SEG, P + 1])
        ss = sb("ss", [P, SEG, P + 1])
        aa = sb("aa", [P, SEG, P + 1])
        tg = sb("tg", [P, SEG, P])
        vs = sb("vs", [P, HALF, W])
        tr = sb("tr", [P, HALF, W])
        yz = sb("yz", [P, HALF, W])
        tc = sb("tc", [P, HALF, W])
        xck_h, xck_l = sb("xck_h", [P, HALF, W], F32R), sb("xck_l", [P, HALF, W], F32R)
        hid = [sb(f"hid{i}", [P, W]) for i in range(2)]
        kc = [sb(f"kc{i}", [P, W]) for i in range(KC)]
        kc_h = [sb(f"kc_h{i}", [P, W], F32R) for i in range(KC)]
        kc_l = [sb(f"kc_l{i}", [P, W], F32R) for i in range(KC)]

        ring = psum("ring", [P, RING, W])
        turn = psum("turn", [P, HALF, W])
        vc = psum("vc", [P, HALF, W])

        x_in = [sem("x_in0"), sem("x_in1")]
        stored = [sem("stored0"), sem("stored1")]
        cols_in, rhs_in = sem("cols_in"), sem("rhs_in")
        kvr_in, cm_in = sem("kvr_in"), sem("cm_in")
        consts_pool, ident_pool, setup_dve, setup_pe = sem("consts_pool"), sem("ident_pool"), sem("setup_dve"), sem("setup_pe")
        ln1_step, ln2_step = sem("ln1_step"), sem("ln2_step")
        rsq1_ok, rsq2_ok = sem("rsq1_ok"), sem("rsq2_ok")
        xz_scales, xz_ok, xn_ok, quant_scales = sem("xz_scales"), sem("xz_ok"), sem("xn_ok"), sem("quant_scales")
        qf_ok, qb_ok, qc_ok, ffn_ok, base0_ok = sem("qf_ok"), sem("qb_ok"), sem("qc_ok"), sem("ffn_ok"), sem("base0_ok")
        t1_done, tq_done, ff_done = sem("t1_done"), sem("tq_done"), sem("ff_done")
        t2_done, t3_done = sem("t2_done"), sem("t3_done")
        xa_ok, xa_carry, dx_ok, xk_ok, xv_ok, xr_ok = (sem(n) for n in ("xa_ok", "xa_carry", "dx_ok", "xk_ok", "xv_ok", "xr_ok"))
        k_done, v_done, r_done = sem("k_done"), sem("v_done"), sem("r_done")
        kt_ok, kt_carry, vs_ok, tr_ok = sem("kt_ok"), sem("kt_carry"), sem("vs_ok"), sem("tr_ok")
        mx_ok, d0_ok, relu_d, em_ok, ek_ok = sem("mx_ok"), sem("d0_ok"), sem("relu_d"), sem("em_ok"), sem("ek_ok")
        s_carry, ss_ok, ln_ok, d_ok = sem("s_carry"), sem("ss_ok"), sem("ln_ok"), sem("d_ok")
        relu_e, e1_ok, e2_ok, tg_ok = sem("relu_e"), sem("e1_ok"), sem("e2_ok"), sem("tg_ok")
        aa_carry, ev_ok, aa_ok, y_step, z_ok = sem("aa_carry"), sem("ev_ok"), sem("aa_ok"), sem("y_step"), sem("z_ok")
        x1_ok, bias2_ok, xbt_ok, xb_ok, xb_carry, dxb_ok = (sem(n) for n in ("x1_ok", "bias2_ok", "xbt_ok", "xb_ok", "xb_carry", "dxb_ok"))
        xck_hi, xck_lo, split_hi, split_lo, staged = sem("xck_hi"), sem("xck_lo"), sem("split_hi"), sem("split_lo"), sem("staged")
        xck_ok, xcr_ok, rc_done, tc_ok = sem("xck_ok"), sem("xcr_ok"), sem("rc_done"), sem("tc_ok")
        h_done, relu_ok, kc_ok, kc_hi, square_ok, kc_lo, vc_step = (sem(n) for n in ("h_done", "relu_ok", "kc_ok", "kc_hi", "square_ok", "kc_lo", "vc_step"))
        z2_ok, base1_ok, out_ok = sem("z2_ok"), sem("base1_ok"), sem("out_ok")

        def back(t, k):
            d = t[1] - k
            return t[0] + d // 2, d % 2

        def known(c):
            return isinstance(c[0], int)

        def exists(c):
            return not known(c) or 0 <= 2 * c[0] + c[1] < N

        def signals(c, per=1, k=None):
            k = per - 1 if k is None else k
            n = 2 * c[0] + c[1]
            return (min(n, N - 1) if known(c) else n) * per + k + 1

        def reached(eng, s, c, per=1, k=None):
            if not known(c) or c[0] >= 0:
                eng.wait_ge(s, signals(c, per, k))

        def reached_dma(eng, sems, c):
            if known(c) and c[0] < 0:
                return
            eng.wait_ge(sems[c[1]], (c[0] + 1) * 16)

        def iterations(eng, step, peeled):
            for t in range(-1, 4):
                peeled.get(t, step)((t // 2, t % 2))
            with eng.Fori(2, N // 2 - 1) as m:
                step((m, 0))
                step((m, 1))
            for t in range(N - 2, N + 2):
                peeled.get(t, step)((t // 2, t % 2))

        def col(name, h):
            i = COLS.index(name)
            return cols_s[:, i, h:h + 1]

        def half(tile, h, a=0, b=P):
            return tile[:, B * h:B * (h + 1), a:b]

        def seg(ap):
            return ap.rearrange("p (b j) -> p b j", b=B)

        x_d = x.rearrange("b (n p) c -> n p b c", p=P)
        out_d = out.rearrange("b (n p) c -> n p b c", p=P)

        ones = tg[:, 0, :]
        rq_amax, rq_scale, rq_inv = (tc[:, 0, HALF * i:HALF * (i + 1)] for i in range(3))
        rhs_s = x1[:, 0:HALF, :]
        landings = [(base1[g][:].rearrange("p b c -> p (b c)"), wck_h[:, g, :], wck_l[:, g, :]) for g in range(HALF)]
        landings.append((base0[1][:], wcv_h[:], wcv_l[:]))
        wcv_d = wcv.rearrange("(i k p) d -> k p i d", k=2, p=P)

        block = ctx.enter_context(nc.Block())

        @block.sync
        def _(sp):
            def load(c):
                sp.dma_start(x_t[c[1]][:], x_d[2 * c[0] + c[1]]).then_inc(x_in[c[1]], 16)

            load((0, 0))
            sp.dma_start(cols_s[:, 0:len(COLS), :], cols.rearrange("p (i h) -> p i h", h=HALF)).then_inc(cols_in, 16)
            load((0, 1))
            for w_d, w_s in ((wk, wk_s), (wv, wv_s), (wr, wr_s)):
                sp.dma_start(w_s[:], w_d.rearrange("(h p) d -> p h d", p=P)).then_inc(kvr_in, 16)

            def step(t):
                ahead = back(t, -2)
                if exists(ahead) and exists(t):
                    reached(sp, base0_ok, t)
                    load(ahead)
                c = back(t, 2)
                if exists(c):
                    reached(sp, out_ok, c)
                    sp.dma_start(out_d[2 * c[0] + c[1]], base1[c[1]][:]).then_inc(stored[c[1]], 16)

            iterations(sp, step, {})
            sp.wait_ge(stored[0], 16 * (N // 2))
            sp.wait_ge(stored[1], 16 * (N // 2))

        @block.gpsimd
        def _(pool):
            pool.memset(ones, 1.0).then_inc(ident_pool, 1)
            pool.memset(neg_half[:], -0.5).then_inc(ident_pool, 1)
            pool.wait_ge(ident_pool, 2)
            pool.affine_select(out=ident[:], in_=ones, compare_op=ALU.is_equal, fill=0.0, base=0,
                               pattern=[[-1, P]], channel_multiplier=1).then_inc(ident_pool, 1)
            pool.memset(xa[1][:, :, P:P + 1], 0.0).then_inc(consts_pool, 1)
            pool.memset(xb[1][:, :, P:P + 1], 0.0).then_inc(consts_pool, 1)
            pool.memset(mx[:, :, P:P + 1], NEG_INF).then_inc(consts_pool, 1)
            pool.memset(ss[:, :, P:P + 1], 1.0).then_inc(consts_pool, 1)
            pool.memset(aa[:, :, P:P + 1], 0.0).then_inc(consts_pool, 1)
            pool.memset(decay[:, :, 0:1], 0.0).then_inc(consts_pool, 1)
            pool.memset(rise[:, :, 0:1], -BIG).then_inc(consts_pool, 1)
            pool.memset(zeros[:], 0.0).then_inc(consts_pool, 1)
            pool.wait_ge(consts_pool, 8)
            def set_up():
                for n, (whole, high, low) in enumerate(landings):
                    pool.wait_ge(split_hi, n + 1)
                    pool.tensor_tensor(low, whole, high.bitcast(F32), ALU.subtract).then_inc(split_lo, 1)
                pool.wait_ge(split_lo, len(landings))

            def carry_xa(a):
                reached(pool, xr_ok, back(a, 2))
                reached(pool, xa_ok, back(a, 1), 2)
                pool.tensor_tensor(xa[a[1]][:, :, 0:1], xa[1 - a[1]][:, :, P:P + 1], zeros[:], ALU.add).then_inc(xa_carry, 1)

            def shift_difference(a):
                pool.wait_ge(xa_ok, signals(a, 2))
                pool.wait_ge(xa_carry, signals(a))
                reached(pool, xr_ok, back(a, 1))
                pool.tensor_tensor(dx[:], xa[a[1]][:, :, 1:P + 1], xa[a[1]][:, :, 0:P], ALU.subtract).then_inc(dx_ok, 1)

            def add_x(a):
                pool.wait_ge(ffn_ok, signals(a))
                reached_dma(pool, x_in, a)
                pool.tensor_tensor(base0[a[1]][:], base0[a[1]][:], x_t[a[1]][:], ALU.add).then_inc(base0_ok, 1)

            def carry_xb(b):
                reached(pool, xck_ok, back(b, 2))
                reached(pool, xb_ok, back(b, 1), 2)
                pool.tensor_tensor(xb[b[1]][:, :, 0:1], xb[1 - b[1]][:, :, P:P + 1], zeros[:], ALU.add).then_inc(xb_carry, 1)

            def root_2(b):
                pool.wait_ge(ln2_step, signals(b, 3))
                pool.tensor_tensor(rsq2[:], pw2[:], neg_half[:, 0:B], ALU.pow).then_inc(rsq2_ok, 1)

            def add_x1(b):
                pool.wait_ge(base0_ok, signals(b))
                pool.wait_ge(x1_ok, signals(b))
                reached_dma(pool, stored, back(b, 2))
                pool.tensor_tensor(base1[b[1]][:], base0[b[1]][:], x1[:], ALU.add).then_inc(base1_ok, 1)

            def root_1(n):
                pool.wait_ge(ln1_step, signals(n, 3))
                reached(pool, xz_ok, back(n, 1))
                pool.tensor_tensor(rsq1[:], pw1[:], neg_half[:], ALU.pow).then_inc(rsq1_ok, 1)

            def step(t):
                nxt, a, b = back(t, -1), t, back(t, 1)
                if exists(a):
                    carry_xa(a)
                if exists(b):
                    carry_xb(b)
                if exists(a):
                    shift_difference(a)
                if exists(nxt):
                    root_1(nxt)
                if exists(b):
                    root_2(b)
                if exists(a):
                    add_x(a)
                if exists(b):
                    add_x1(b)

            def first(t):
                nxt, a = back(t, -1), t
                carry_xa(a)
                root_1(nxt)
                shift_difference(a)
                set_up()
                add_x(a)

            def second(t):
                nxt, a, b = back(t, -1), t, back(t, 1)
                carry_xa(a)
                carry_xb(b)
                root_1(nxt)
                shift_difference(a)
                root_2(b)
                add_x1(b)
                add_x(a)

            def last_but_one(t):
                b = back(t, 1)
                root_2(b)
                add_x1(b)
                carry_xb(b)

            iterations(pool, step, {0: first, 1: second, N: last_but_one})

        @block.scalar
        def _(act):
            act.dma_start(rhs_s, rhs.rearrange("(h p) d -> p h d", p=P)).then_inc(rhs_in, 16)
            for g in range(HALF):
                act.dma_start(landings[g][0], wck[g * P:(g + 1) * P, :]).then_inc(staged, 16)
            act.dma_start(landings[HALF][0], wcv_d[0]).then_inc(staged, 16)
            act.dma_start(wcr_s[:], wcr.rearrange("(h p) d -> p h d", p=P)).then_inc(cm_in, 16)
            act.dma_start(wcv_s[:], wcv_d[1]).then_inc(cm_in, 16)
            act.wait_ge(consts_pool, 8)
            act.wait_ge(cols_in, 16)

            def set_up():
                act.wait_ge(staged, 16 * len(landings))
                for whole, high, _ in landings:
                    act.activation(high, whole, ACT.Copy).then_inc(split_hi, 1)

            def gate_c(c, h):
                act.wait_ge(rc_done, signals(c, HALF, h))
                if h == 0:
                    reached(act, out_ok, back(c, 1))
                act.activation(tc[:, h, :], ring[:, h, :], ACT.Tanh, scale=0.5).then_inc(tc_ok, 1)

            def hidden(c, j):
                act.wait_ge(h_done, signals(c, HT, j))
                reached(act, kc_ok if j % 2 else kc_lo, c if j >= 2 else back(c, 1), PAIRS, (j // 2 - 1) % PAIRS)
                act.activation(hid[j % 2][:], ring[:, (2 + j) % RING, :], ACT.Relu).then_inc(relu_ok, 1)

            def squares(c, j):
                i = j // 2
                act.wait_ge(relu_ok, signals(c, HT, j))
                reached(act, vc_step, c if i >= KC else back(c, 1), HT, (j - 2 * KC) % HT)
                if j % 2:
                    act.activation(kc[i % KC][:], hid[1][:], ACT.Square).then_inc(kc_ok, 1)
                else:
                    act.activation(kc_h[i % KC][:], hid[0][:], ACT.Square).then_inc(kc_hi, 1)
                    act.wait_ge(kc_hi, signals(c, PAIRS, i))
                    act.activation(hid[0][:], hid[0][:], ACT.Square).then_inc(square_ok, 1)

            def norm_z(a):
                act.wait_ge(xz_scales, signals(a))
                reached(act, t3_done, back(a, 2))
                reached(act, t1_done, back(a, 1))
                for b in range(B):
                    i = act.activation(nrm[:, b, :], x_t[a[1]][:, b, :], ACT.Identity,
                                       scale=rsq1[:, B + b:B + b + 1], bias=bias_z[:, b:b + 1])
                i.then_inc(xz_ok, 1)

            def falls(c, ready, relus):
                act.wait_ge(ready, signals(c))
                act.activation(decay[:, :, 1:P + 1], dd[:], ACT.Relu).then_inc(relus, 1)
                act.activation(inject[:, :, 1:P + 1], dd[:], ACT.Relu, scale=-1.0).then_inc(relus, 1)

            def exps(c, relus, low_ok, high_ok):
                act.wait_ge(relus, signals(c, 2, 0))
                act.activation(decay[:, :, 1:P + 1], decay[:, :, 1:P + 1], ACT.Exp, scale=-1.0).then_inc(low_ok, 1)
                act.wait_ge(relus, signals(c, 2, 1))
                act.activation(inject[:, :, 1:P + 1], inject[:, :, 1:P + 1], ACT.Exp, scale=-1.0).then_inc(high_ok, 1)

            def key(a, b, h):
                reached(act, d_ok, b)
                act.wait_ge(k_done, signals(a, HALF, h))
                act.activation(half(kt, h, 1, P + 1), seg(ring[:, (10 + h) % RING, :]), ACT.Copy).then_inc(kt_ok, 1)

            def quant(a):
                act.wait_ge(quant_scales, signals(a, 3))
                reached(act, qb_ok, back(a, 1))
                for b in range(B):
                    i = act.activation(q_f[:, b, :], xn[a[1]][:, b, :], ACT.Copy, scale=lhs_inv[:, b:b + 1], bias=MAGIC)
                i.then_inc(qf_ok, 1)

            def evac_xa(a):
                act.wait_ge(t1_done, signals(a))
                reached(act, xr_ok, back(a, 2))
                reached(act, xa_carry, back(a, 1))
                for h in range(HALF):
                    act.activation(half(xa[a[1]], h, 1, P + 1), seg(turn[:, h, :]), ACT.Identity,
                                   scale=col("g1", h), bias=col("b1", h)).then_inc(xa_ok, 1)

            def evac_xb(b):
                act.wait_ge(t3_done, signals(b))
                reached(act, xck_ok, back(b, 2))
                reached(act, xb_carry, back(b, 1))
                for h in range(HALF):
                    act.activation(half(xb[b[1]], h, 1, P + 1), seg(turn[:, h, :]), ACT.Identity,
                                   scale=col("g2", h), bias=col("b2", h)).then_inc(xb_ok, 1)

            def value(a, b, h):
                if h == 0:
                    reached(act, y_step, b, 3, 0)
                act.wait_ge(v_done, signals(a, HALF, h))
                act.activation(vs[:, h, :], ring[:, (12 + h) % RING, :], ACT.Copy).then_inc(vs_ok, 1)

            def gate_r(a, b, h):
                if h == 0:
                    reached(act, z_ok, b)
                act.wait_ge(r_done, signals(a, HALF, h))
                act.activation(tr[:, h, :], ring[:, (14 + h) % RING, :], ACT.Tanh, scale=0.5).then_inc(tr_ok, 1)

            def ln_s(b):
                act.wait_ge(ss_ok, signals(b))
                act.activation(kt[:, :, 0:P], ss[:, :, 0:P], ACT.Ln).then_inc(ln_ok, 1)

            def gate_u(b):
                reached(act, z_ok, back(b, 1))
                for h in range(HALF):
                    i = act.activation(half(tg, h), half(dd, h), ACT.Tanh, scale=0.5, bias=half_u[:, h:h + 1])
                i.then_inc(tg_ok, 1)

            def norm_x1(a, b):
                reached(act, bias2_ok, b)
                act.wait_ge(t1_done, signals(a))
                for s in range(B):
                    i = act.activation(nrm[:, s, :], x1[:, s, :], ACT.Identity,
                                       scale=rsq2[:, s:s + 1], bias=bias_2[:, s:s + 1])
                i.then_inc(xbt_ok, 1)

            def xck_high(b, c):
                act.wait_ge(xck_ok, signals(b))
                reached(act, h_done, c, HT)
                act.activation(xck_h[:], xck[:], ACT.Copy).then_inc(xck_hi, 1)

            def step(t):
                nxt, a, b, c = back(t, -1), t, back(t, 1), back(t, 2)
                if exists(c):
                    gate_c(c, 0)
                    gate_c(c, 1)
                if exists(b):
                    ln_s(b)
                if exists(c):
                    hidden(c, 0)
                    hidden(c, 1)
                    squares(c, 0)
                if exists(a):
                    evac_xa(a)
                if exists(c):
                    squares(c, 1)
                if exists(b):
                    falls(b, d_ok, relu_e)
                    exps(b, relu_e, e1_ok, e2_ok)
                if exists(c):
                    hidden(c, 2)
                    hidden(c, 3)
                    squares(c, 2)
                if exists(b):
                    gate_u(b)
                if exists(c):
                    hidden(c, 4)
                    squares(c, 3)
                    hidden(c, 5)
                    squares(c, 4)
                    hidden(c, 6)
                    squares(c, 5)
                    squares(c, 6)
                if exists(a):
                    key(a, b, 0)
                    key(a, b, 1)
                if exists(c):
                    hidden(c, 7)
                if exists(a):
                    value(a, b, 0)
                if exists(c):
                    squares(c, 7)
                if exists(b):
                    norm_x1(a, b)
                if exists(a):
                    falls(a, d0_ok, relu_d)
                if exists(b):
                    evac_xb(b)
                if exists(nxt):
                    norm_z(nxt)
                if exists(a):
                    exps(a, relu_d, em_ok, ek_ok)
                if exists(b):
                    xck_high(b, c)
                if exists(a):
                    gate_r(a, b, 0)
                    gate_r(a, b, 1)
                    value(a, b, 1)
                if exists(nxt):
                    quant(nxt)

            def first(t):
                nxt, a, b = back(t, -1), t, back(t, 1)
                evac_xa(a)
                set_up()
                norm_z(nxt)
                key(a, b, 0)
                key(a, b, 1)
                quant(nxt)
                value(a, b, 0)
                falls(a, d0_ok, relu_d)
                exps(a, relu_d, em_ok, ek_ok)
                value(a, b, 1)
                gate_r(a, b, 0)
                gate_r(a, b, 1)

            def second(t):
                nxt, a, b, c = back(t, -1), t, back(t, 1), back(t, 2)
                ln_s(b)
                evac_xa(a)
                falls(b, d_ok, relu_e)
                exps(b, relu_e, e1_ok, e2_ok)
                gate_u(b)
                key(a, b, 0)
                key(a, b, 1)
                value(a, b, 0)
                value(a, b, 1)
                gate_r(a, b, 0)
                norm_x1(a, b)
                quant(nxt)
                evac_xb(b)
                falls(a, d0_ok, relu_d)
                exps(a, relu_d, em_ok, ek_ok)
                gate_r(a, b, 1)
                xck_high(b, c)
                norm_z(nxt)

            def last_but_one(t):
                a, b, c = t, back(t, 1), back(t, 2)
                gate_c(c, 0)
                ln_s(b)
                gate_c(c, 1)
                falls(b, d_ok, relu_e)
                exps(b, relu_e, e1_ok, e2_ok)
                hidden(c, 0)
                squares(c, 0)
                hidden(c, 1)
                gate_u(b)
                hidden(c, 2)
                squares(c, 1)
                squares(c, 2)
                hidden(c, 3)
                squares(c, 3)
                hidden(c, 4)
                squares(c, 4)
                hidden(c, 5)
                squares(c, 5)
                hidden(c, 6)
                norm_x1(a, b)
                squares(c, 6)
                evac_xb(b)
                hidden(c, 7)
                squares(c, 7)
                xck_high(b, c)

            def last(t):
                c = back(t, 2)
                gate_c(c, 0)
                gate_c(c, 1)
                hidden(c, 0)
                squares(c, 0)
                hidden(c, 1)
                hidden(c, 2)
                squares(c, 1)
                hidden(c, 3)
                squares(c, 2)
                hidden(c, 4)
                squares(c, 3)
                squares(c, 4)
                hidden(c, 5)
                hidden(c, 6)
                squares(c, 5)
                hidden(c, 7)
                squares(c, 6)
                squares(c, 7)

            iterations(act, step, {0: first, 1: second, N: last_but_one, N + 1: last})

        @block.vector
        def _(dve):
            dve.wait_ge(ident_pool, 3)
            dve.tensor_copy(ident_b[:], ident[:]).then_inc(setup_dve, 1)

            def set_up():
                dve.wait_ge(cols_in, 16)
                dve.wait_ge(setup_pe, 1)
                dve.tensor_reduce(rq_amax, vc[:, :, 0:C], AX.X, ALU.max,
                                  apply_absolute_value=True).then_inc(setup_dve, 1)
                dve.wait_ge(setup_dve, 2)
                dve.tensor_scalar(rq_scale, rq_amax, 1e-12, 1.0 / INT8_MAX, ALU.max, ALU.mult).then_inc(setup_dve, 1)
                dve.wait_ge(setup_dve, 3)
                dve.reciprocal(rq_inv, rq_scale[:]).then_inc(setup_dve, 1)
                dve.wait_ge(setup_dve, 4)
                for h in range(HALF):
                    dve.tensor_scalar(yz[:, h, 0:C], vc[:, h, 0:C], rq_inv[:, h:h + 1], MAGIC, ALU.mult, ALU.add)
                    dve.tensor_scalar(tr[:, h, 0:P], ident[:], rq_scale[:, h:h + 1], None, ALU.mult).then_inc(setup_dve, 1)
                dve.wait_ge(setup_dve, 6)
                dve.tensor_scalar(rhs_q[:], yz[:, :, 0:C], MAGIC + INT8_MAX, MAGIC,
                                  ALU.min, ALU.subtract).then_inc(setup_dve, 1)
                for h in range(HALF):
                    dve.tensor_scalar(half(rise, h, 1, P + 1), ones.unsqueeze(1).broadcast_to([P, B, P]), col("w", h),
                                      None, ALU.mult).then_inc(setup_dve, 1)
                dve.tensor_scalar(half_u, cols_s[:, COLS.index("u"), :], 0.5, None, ALU.mult).then_inc(setup_dve, 1)
                dve.wait_ge(setup_pe, 2)
                dve.tensor_scalar(rhs_q[:], ring[:, 0, :].bitcast(BF16)[:, 0:HALF * C].rearrange("p (h d) -> p h d", h=HALF),
                                  -INT8_MAX, None, ALU.max).then_inc(setup_dve, 1)
                dve.tensor_copy(rhs_scale[:], ring[:, 1, 0:C]).then_inc(setup_dve, 1)
                dve.wait_ge(consts_pool, 8)
                dve.wait_ge(setup_dve, 12)

            y_c = yz[:].rearrange("p h (b j) -> p (h b) j", b=B)

            def stats(tile, st, steps):
                for s in range(B):
                    i = dve.bn_stats(st[:, s, :], tile[:, s, :])
                i.then_inc(steps, 1)

            def moments(st, mv, steps, c):
                reached(dve, steps, c, 3, 0)
                dve.tensor_copy(count[:, 0:1], st[:, 0, 0:1])
                for s in range(B):
                    i = dve.bn_aggr(mv[:, s, :], st[:, s, :])
                i.then_inc(steps, 1)
                reached(dve, steps, c, 3, 1)

            def stats_1(a):
                reached_dma(dve, x_in, a)
                stats(x_t[a[1]], st1, ln1_step)

            def moments_1(a):
                moments(st1, mv1, ln1_step, a)
                dve.tensor_scalar(pw1[:, 0:B], mv1[:, :, 1], EPS, None, ALU.add)
                dve.tensor_scalar(pw1[:, B:2 * B], mv1[:, :, 1], 1.0 + EPS, EPS * EPS, ALU.mult, ALU.add).then_inc(ln1_step, 1)

            def carry_max(a):
                reached(dve, d_ok, back(a, 1))
                dve.tensor_copy(kt[:, :, 0:1], mx[:, :, P:P + 1]).then_inc(kt_carry, 1)

            def running_max(a):
                dve.wait_ge(kt_ok, signals(a, HALF))
                dve.wait_ge(kt_carry, signals(a))
                dve.tensor_tensor_scan(mx[:].rearrange("p s j -> p (s j)"), rise[:].rearrange("p s j -> p (s j)"),
                                       kt[:].rearrange("p s j -> p (s j)"), 0.0, ALU.add, ALU.max).then_inc(mx_ok, 1)

            def log_ratio_0(a):
                dve.wait_ge(mx_ok, signals(a))
                for h in range(HALF):
                    i = dve.scalar_tensor_tensor(half(dd, h), half(kt, h, 1, P + 1), col("w", h), half(mx, h),
                                                 ALU.subtract, ALU.subtract)
                i.then_inc(d0_ok, 1)

            def bias_1(a):
                dve.wait_ge(rsq1_ok, signals(a))
                dve.scalar_tensor_tensor(bias_z[:], mv1[:, :, 0], -1.0, rsq1[:, B:2 * B], ALU.mult,
                                         ALU.mult).then_inc(xz_scales, 1)

            def norm_1(a):
                dve.wait_ge(rsq1_ok, signals(a))
                reached(dve, qf_ok, back(a, 1))
                reached(dve, x1_ok, back(a, 2))
                for s in range(B):
                    i = dve.tensor_scalar(xn[a[1]][:, s, :], x_t[a[1]][:, s, :], mv1[:, s, 0:1], rsq1[:, s:s + 1],
                                          ALU.subtract, ALU.mult)
                i.then_inc(xn_ok, 1)

            def largest(a):
                dve.wait_ge(xn_ok, signals(a))
                dve.tensor_reduce(amax[:], xn[a[1]][:], AX.X, ALU.max, apply_absolute_value=True).then_inc(quant_scales, 1)

            def scales_q(a):
                dve.wait_ge(quant_scales, signals(a, 3, 0))
                dve.tensor_scalar(lhs_scale[a[1]][:], amax[:], 1e-12, 1.0 / INT8_MAX, ALU.max, ALU.mult).then_inc(quant_scales, 1)
                dve.wait_ge(quant_scales, signals(a, 3, 1))
                reached(dve, qf_ok, back(a, 1))
                dve.reciprocal(lhs_inv[:], lhs_scale[a[1]][:]).then_inc(quant_scales, 1)

            def carry_s(b):
                reached(dve, aa_ok, back(b, 1))
                dve.tensor_copy(inject[:, :, 0:1], ss[:, :, P:P + 1]).then_inc(s_carry, 1)

            def scan_s(b):
                dve.wait_ge(em_ok, signals(b))
                dve.wait_ge(ek_ok, signals(b))
                dve.wait_ge(s_carry, signals(b))
                dve.tensor_tensor_scan(ss[:].rearrange("p s j -> p (s j)"), decay[:].rearrange("p s j -> p (s j)"),
                                       inject[:].rearrange("p s j -> p (s j)"), 0.0, ALU.mult, ALU.add).then_inc(ss_ok, 1)

            def round_q(a):
                dve.wait_ge(qf_ok, signals(a))
                reached(dve, tq_done, back(a, 1))
                dve.tensor_scalar(q_b[:], q_f[:], MAGIC + INT8_MAX, MAGIC, ALU.min, ALU.subtract).then_inc(qb_ok, 1)

            def log_ratio(b):
                dve.wait_ge(ln_ok, signals(b))
                dve.tensor_tensor(dd[:], dd[:], kt[:, :, 0:P], ALU.subtract).then_inc(d_ok, 1)

            def evac_q(a):
                dve.wait_ge(tq_done, signals(a))
                reached(dve, ff_done, back(a, 1))
                dve.tensor_scalar(q_c[:], turn[:, 0, :].bitcast(BF16).rearrange("p (h w) -> p h w", h=HALF),
                                  -INT8_MAX, None, ALU.max).then_inc(qc_ok, 1)

            def token_mix(a, name, tile, done, ok):
                dve.wait_ge(dx_ok, signals(a))
                reached(dve, done, back(a, 1), HALF)
                for h in range(HALF):
                    i = dve.scalar_tensor_tensor(seg(tile[:, h, :]), half(dx, h), col(name, h), half(xa[a[1]], h),
                                                 ALU.mult, ALU.add)
                i.then_inc(ok, 1)

            def carry_aa(b):
                dve.wait_ge(ss_ok, signals(b))
                dve.tensor_copy(inject[:, :, 0:1], aa[:, :, P:P + 1]).then_inc(aa_carry, 1)

            def weigh_values(b):
                dve.wait_ge(e2_ok, signals(b))
                dve.wait_ge(vs_ok, signals(b, HALF))
                dve.tensor_tensor(inject[:, :, 1:P + 1], inject[:, :, 1:P + 1],
                                  vs[:].rearrange("p h (b j) -> p (h b) j", b=B), ALU.mult).then_inc(ev_ok, 1)

            def scan_aa(b):
                dve.wait_ge(aa_carry, signals(b))
                dve.wait_ge(ev_ok, signals(b))
                dve.wait_ge(e1_ok, signals(b))
                dve.tensor_tensor_scan(aa[:].rearrange("p s j -> p (s j)"), decay[:].rearrange("p s j -> p (s j)"),
                                       inject[:].rearrange("p s j -> p (s j)"), 0.0, ALU.mult, ALU.add).then_inc(aa_ok, 1)

            def value_step(b):
                dve.wait_ge(aa_ok, signals(b))
                reached(dve, t2_done, back(b, 1))
                dve.tensor_tensor(y_c, vs[:].rearrange("p h (b j) -> p (h b) j", b=B), aa[:, :, 0:P],
                                  ALU.subtract).then_inc(y_step, 1)

            def weighted_step(b):
                dve.wait_ge(y_step, signals(b, 3, 0))
                dve.wait_ge(tg_ok, signals(b))
                dve.scalar_tensor_tensor(y_c, tg[:], 1.0, y_c, ALU.add, ALU.mult).then_inc(y_step, 1)

            def whole_step(b):
                dve.wait_ge(y_step, signals(b, 3, 1))
                dve.scalar_tensor_tensor(y_c, aa[:, :, 0:P], 2.0, y_c, ALU.mult, ALU.add).then_inc(y_step, 1)

            def gated(b):
                dve.wait_ge(y_step, signals(b, 3, 2))
                dve.wait_ge(tr_ok, signals(b, HALF))
                dve.scalar_tensor_tensor(yz[:], tr[:], 1.0, yz[:], ALU.add, ALU.mult).then_inc(z_ok, 1)

            def scaled_product(a):
                dve.wait_ge(ff_done, signals(a))
                reached(dve, base1_ok, back(a, 2))
                for s in range(B):
                    i = dve.scalar_tensor_tensor(base0[a[1]][:, s, :], turn[:, s // 2, (s % 2) * C:(s % 2 + 1) * C],
                                                 lhs_scale[a[1]][:, s:s + 1], rhs_scale[:], ALU.mult, ALU.mult)
                i.then_inc(ffn_ok, 1)

            def residual_1(b):
                dve.wait_ge(t2_done, signals(b))
                reached(dve, base1_ok, back(b, 1))
                reached(dve, xbt_ok, back(b, 1))
                dve.scalar_tensor_tensor(x1[:].rearrange("p b c -> p (b c)"), turn[:].rearrange("p h w -> p (h w)"), 0.25,
                                         xn[b[1]][:].rearrange("p b c -> p (b c)"), ALU.mult, ALU.add).then_inc(x1_ok, 1)

            def stats_2(b):
                dve.wait_ge(x1_ok, signals(b))
                stats(x1, st2, ln2_step)

            def moments_2(b):
                moments(st2, mv2, ln2_step, b)
                dve.tensor_scalar(pw2[:], mv2[:, :, 1], EPS, None, ALU.add).then_inc(ln2_step, 1)

            def mix_to(b, name, tile, done, per, ok):
                dve.wait_ge(dxb_ok, signals(b))
                reached(dve, done, back(b, 1), per)
                for h in range(HALF):
                    i = dve.scalar_tensor_tensor(seg(tile[:, h, :]), half(dxb, h), col(name, h), half(xb[b[1]], h),
                                                 ALU.mult, ALU.add)
                i.then_inc(ok, 1)

            def shift_difference(b):
                dve.wait_ge(xb_ok, signals(b, 2))
                dve.wait_ge(xb_carry, signals(b))
                dve.tensor_tensor(dxb[:], xb[b[1]][:, :, 1:P + 1], xb[b[1]][:, :, 0:P], ALU.subtract).then_inc(dxb_ok, 1)

            def receptance_mix(b):
                mix_to(b, "crr", xcr, rc_done, HALF, xcr_ok)

            def key_mix(b):
                mix_to(b, "crk", xck, h_done, HT, xck_ok)

            def xck_low(b):
                dve.wait_ge(xck_hi, signals(b))
                dve.tensor_tensor(xck_l[:], xck[:], xck_h[:].bitcast(F32), ALU.subtract).then_inc(xck_lo, 1)

            def hidden_low(c, j):
                i = j // 2
                dve.wait_ge(square_ok, signals(c, PAIRS, i))
                reached(dve, vc_step, c if i >= KC else back(c, 1), HT, (j - 2 * KC) % HT)
                dve.tensor_tensor(kc_l[i % KC][:], hid[0][:], kc_h[i % KC][:].bitcast(F32), ALU.subtract).then_inc(kc_lo, 1)

            def value_gated(c):
                dve.wait_ge(vc_step, signals(c, HT))
                dve.wait_ge(tc_ok, signals(c, HALF))
                dve.scalar_tensor_tensor(tc[:], tc[:], 1.0, vc[:], ALU.add, ALU.mult).then_inc(z2_ok, 1)

            def result(c):
                dve.wait_ge(z2_ok, signals(c))
                dve.wait_ge(base1_ok, signals(c))
                o = base1[c[1]][:].rearrange("p b c -> p (b c)")
                dve.scalar_tensor_tensor(o, tc[:].rearrange("p h w -> p (h w)"), 0.5, o, ALU.mult,
                                         ALU.add).then_inc(out_ok, 1)

            def bias2(b):
                dve.wait_ge(rsq2_ok, signals(b))
                dve.scalar_tensor_tensor(bias_2[:], mv2[:, :, 0], -1.0, rsq2[:], ALU.mult,
                                         ALU.mult).then_inc(bias2_ok, 1)

            def step(t):
                nxt, a, b, c = back(t, -1), t, back(t, 1), back(t, 2)
                if exists(b):
                    carry_s(b)
                    scan_s(b)
                if exists(a):
                    round_q(a)
                if exists(b):
                    carry_aa(b)
                if exists(a):
                    evac_q(a)
                if exists(b):
                    log_ratio(b)
                if exists(nxt):
                    stats_1(nxt)
                if exists(c):
                    hidden_low(c, 0)
                if exists(nxt):
                    moments_1(nxt)
                if exists(a):
                    scaled_product(a)
                    carry_max(a)
                    token_mix(a, "rk", xk, k_done, xk_ok)
                    token_mix(a, "rv", xv, v_done, xv_ok)
                if exists(b):
                    weigh_values(b)
                    scan_aa(b)
                if exists(c):
                    hidden_low(c, 2)
                if exists(b):
                    value_step(b)
                    weighted_step(b)
                    whole_step(b)
                    gated(b)
                if exists(c):
                    hidden_low(c, 4)
                if exists(b):
                    residual_1(b)
                    stats_2(b)
                    moments_2(b)
                if exists(nxt):
                    bias_1(nxt)
                if exists(a):
                    running_max(a)
                if exists(b):
                    bias2(b)
                if exists(c):
                    hidden_low(c, 6)
                if exists(a):
                    log_ratio_0(a)
                if exists(nxt):
                    norm_1(nxt)
                if exists(a):
                    token_mix(a, "rr", xr, r_done, xr_ok)
                if exists(nxt):
                    largest(nxt)
                if exists(b):
                    shift_difference(b)
                if exists(nxt):
                    scales_q(nxt)
                if exists(b):
                    key_mix(b)
                    receptance_mix(b)
                if exists(c):
                    value_gated(c)
                if exists(b):
                    xck_low(b)
                if exists(c):
                    result(c)

            def first(t):
                nxt, a = back(t, -1), t
                stats_1(nxt)
                round_q(a)
                moments_1(nxt)
                carry_max(a)
                evac_q(a)
                set_up()
                norm_1(nxt)
                token_mix(a, "rk", xk, k_done, xk_ok)
                bias_1(nxt)
                largest(nxt)
                token_mix(a, "rv", xv, v_done, xv_ok)
                scaled_product(a)
                scales_q(nxt)
                running_max(a)
                log_ratio_0(a)
                token_mix(a, "rr", xr, r_done, xr_ok)

            def second(t):
                nxt, a, b = back(t, -1), t, back(t, 1)
                stats_1(nxt)
                carry_s(b)
                round_q(a)
                scan_s(b)
                moments_1(nxt)
                evac_q(a)
                carry_aa(b)
                log_ratio(b)
                carry_max(a)
                scaled_product(a)
                token_mix(a, "rk", xk, k_done, xk_ok)
                token_mix(a, "rv", xv, v_done, xv_ok)
                weigh_values(b)
                scan_aa(b)
                value_step(b)
                weighted_step(b)
                whole_step(b)
                bias_1(nxt)
                gated(b)
                token_mix(a, "rr", xr, r_done, xr_ok)
                residual_1(b)
                stats_2(b)
                moments_2(b)
                norm_1(nxt)
                bias2(b)
                largest(nxt)
                scales_q(nxt)
                running_max(a)
                log_ratio_0(a)
                shift_difference(b)
                receptance_mix(b)
                key_mix(b)
                xck_low(b)

            def last_but_one(t):
                b, c = back(t, 1), back(t, 2)
                carry_s(b)
                scan_s(b)
                log_ratio(b)
                carry_aa(b)
                weigh_values(b)
                scan_aa(b)
                hidden_low(c, 0)
                value_step(b)
                weighted_step(b)
                whole_step(b)
                gated(b)
                hidden_low(c, 2)
                residual_1(b)
                stats_2(b)
                moments_2(b)
                hidden_low(c, 4)
                bias2(b)
                hidden_low(c, 6)
                shift_difference(b)
                receptance_mix(b)
                key_mix(b)
                value_gated(c)
                xck_low(b)
                result(c)

            def last(t):
                c = back(t, 2)
                hidden_low(c, 0)
                hidden_low(c, 2)
                hidden_low(c, 4)
                hidden_low(c, 6)
                value_gated(c)
                result(c)

            iterations(dve, step, {0: first, 1: second, N: last_but_one, N + 1: last})

        @block.tensor
        def _(pe):
            pe.wait_ge(ident_pool, 3)
            pe.wait_ge(rhs_in, 16)
            for h in range(HALF):
                for g in range(HALF):
                    i = pe.transpose(vc[:, h, g * P:(g + 1) * P], rhs_s[:, g, h * P:(h + 1) * P], ident[:])
            i.then_inc(setup_pe, 1)
            pe.wait_ge(setup_dve, 1)

            def set_up():
                pe.wait_ge(setup_dve, 7)
                for h in range(HALF):
                    pe.matmul(ring[:, 1, h * P:(h + 1) * P], ones, tr[:, h, 0:P], start=True, stop=True)
                for g in range(HALF):
                    for h in range(HALF):
                        i = pe.transpose(ring[:, 0, :].bitcast(BF16)[:, g * C + h * P:g * C + (h + 1) * P],
                                         rhs_q[:, h, g * P:(g + 1) * P], ident_b[:])
                i.then_inc(setup_pe, 1)

            def project(bank, weights, act_tile, o):
                for g in range(HALF):
                    i = pe.matmul(ring[:, bank, :], weights[:, g, o * P:(o + 1) * P], act_tile[:, g, :],
                                  start=(g == 0), stop=(g == HALF - 1))
                return i

            def project3(bank, weights, act_tile, o):
                terms = [(w, x, g) for w, x in ((0, 0), (1, 0), (0, 1)) for g in range(HALF)]
                for n, (w, x, g) in enumerate(terms):
                    i = pe.matmul(ring[:, bank, :], weights[w][:, g, o * P:(o + 1) * P], act_tile[x][:, g, :],
                                  start=(n == 0), stop=(n == len(terms) - 1))
                return i

            def gate_c(c, t, h):
                if h == 0:
                    pe.wait_ge(xcr_ok, signals(c))
                reached(pe, vs_ok, back(t, 1), HALF, h)
                if known(t):
                    reached(pe, relu_ok, back(c, 1), HT, 6 + h)
                for s in range(2):
                    for g in range(HALF):
                        i = pe.matmul(ring[:, h, s * C:(s + 1) * C], xcr[:, g, (2 * h + s) * P:(2 * h + s + 1) * P],
                                      wcr_s[:, g, :], start=(g == 0), stop=(g == HALF - 1))
                i.then_inc(rc_done, 1)

            def hidden(c, j, t):
                if j == 0:
                    pe.wait_ge(xck_lo, signals(c))
                if j < 2:
                    reached(pe, tr_ok, back(t, 1), HALF, j)
                    if known(t):
                        reached(pe, relu_ok, back(c, 1), HT, 4 + j)
                elif j < 4:
                    pe.wait_ge(tc_ok, signals(c, HALF, j - 2))
                else:
                    pe.wait_ge(relu_ok, signals(c, HT, j - 4))
                project3((2 + j) % RING, (wck_h, wck_l), (xck_h, xck_l), j).then_inc(h_done, 1)

            def value_c(c, j):
                n = j // 2
                if j % 2:
                    pe.wait_ge(kc_ok, signals(c, PAIRS, n))
                    terms = ((kc[n % KC], wcv_s),)
                else:
                    pe.wait_ge(kc_lo, signals(c, PAIRS, n))
                    terms = ((kc_h[n % KC], wcv_h), (kc_h[n % KC], wcv_l), (kc_l[n % KC], wcv_h))
                if j == 0:
                    reached(pe, z2_ok, back(c, 1))
                for s in range(B):
                    for k, (hidden_tile, w) in enumerate(terms):
                        i = pe.matmul(vc[:, s // 2, (s % 2) * C:(s % 2 + 1) * C], hidden_tile[:, s * P:(s + 1) * P],
                                      w[:, n, :], start=(j == 0 and k == 0 and s % 2 == 0),
                                      stop=(j == HT - 1 and s % 2 == 1))
                i.then_inc(vc_step, 1)

            def peeled_waits(a, c):
                if exists(c):
                    pe.wait_ge(cm_in, 32)
                    pe.wait_ge(split_lo, len(landings))
                reached(pe, ffn_ok, back(a, 1))
                reached(pe, xb_ok, back(a, 2), 2)

            def to_channels(src, done, last=None):
                for h in range(HALF):
                    for s in range(B):
                        i = pe.transpose(turn[:, h, s * P:(s + 1) * P], src[:, s, h * P:(h + 1) * P], ident[:])
                i.then_inc(done, 1)

            def to_tokens(src, done):
                for s in range(B):
                    for h in range(HALF):
                        o = (s % 2) * C + h * P
                        i = pe.transpose(turn[:, s // 2, o:o + P], src[:, h, s * P:(s + 1) * P], ident[:])
                i.then_inc(done, 1)

            def turn_1(a):
                pe.wait_ge(xz_ok, signals(a))
                pe.wait_ge(qc_ok, signals(a))
                to_channels(nrm, t1_done)

            def turn_q(a):
                pe.wait_ge(qb_ok, signals(a))
                reached(pe, xb_ok, back(a, 2), 2)
                for h in range(HALF):
                    for s in range(B):
                        o = h * W + s * P
                        i = pe.transpose(turn[:, 0, :].bitcast(BF16)[:, o:o + P], q_b[:, s, h * P:(h + 1) * P], ident_b[:])
                i.then_inc(tq_done, 1)

            def product_q(a):
                pe.wait_ge(xa_ok, signals(a, 2))
                if known(a):
                    pe.wait_ge(setup_dve, 12)
                for s in range(B):
                    for h in range(HALF):
                        i = pe.matmul(turn[:, s // 2, (s % 2) * C:(s % 2 + 1) * C], q_c[:, h, s * P:(s + 1) * P],
                                      rhs_q[:, h, :], start=(h == 0), stop=(h == HALF - 1))
                i.then_inc(ff_done, 1)

            def key(a, c, h):
                pe.wait_ge(xk_ok, signals(a))
                if known(a):
                    pe.wait_ge(kvr_in, 48)
                reached(pe, relu_ok, c, HT, 4 + h)
                if known(a):
                    reached(pe, tr_ok, back(a, 1), HALF, h)
                project((10 + h) % RING, wk_s, xk, h).then_inc(k_done, 1)

            def value(a, c, h):
                pe.wait_ge(xv_ok, signals(a))
                if known(a):
                    pe.wait_ge(setup_dve, 12)
                reached(pe, relu_ok, c, HT, 6 + h)
                if known(a):
                    reached(pe, vs_ok, back(a, 1), HALF, h)
                project((12 + h) % RING, wv_s, xv, h).then_inc(v_done, 1)

            def receptance(a, h):
                pe.wait_ge(xr_ok, signals(a))
                pe.wait_ge(kt_ok, signals(a, HALF, h))
                project((14 + h) % RING, wr_s, xr, h).then_inc(r_done, 1)

            def turn_2(a, b):
                reached(pe, z_ok, b)
                pe.wait_ge(ffn_ok, signals(a))
                to_tokens(yz, t2_done)

            def turn_3(b):
                pe.wait_ge(xbt_ok, signals(b))
                pe.wait_ge(x1_ok, signals(b))
                to_channels(nrm, t3_done)

            def step(t):
                a, b, c = t, back(t, 1), back(t, 2)
                if known(t):
                    peeled_waits(a, c)
                if exists(c):
                    gate_c(c, t, 0)
                    gate_c(c, t, 1)
                    hidden(c, 0, t)
                if exists(a):
                    turn_q(a)
                if exists(c):
                    hidden(c, 1, t)
                if exists(a):
                    turn_1(a)
                if exists(c):
                    hidden(c, 2, t)
                    hidden(c, 3, t)
                if exists(a):
                    product_q(a)
                if exists(c):
                    value_c(c, 0)
                    value_c(c, 1)
                    hidden(c, 4, t)
                    hidden(c, 5, t)
                    hidden(c, 6, t)
                    hidden(c, 7, t)
                    value_c(c, 2)
                if exists(a):
                    key(a, c, 0)
                    key(a, c, 1)
                if exists(b):
                    turn_2(a, b)
                if exists(c):
                    value_c(c, 3)
                if exists(a):
                    value(a, c, 0)
                if exists(c):
                    value_c(c, 4)
                    value_c(c, 5)
                    value_c(c, 6)
                if exists(b):
                    turn_3(b)
                if exists(c):
                    value_c(c, 7)
                if exists(a):
                    value(a, c, 1)
                    receptance(a, 0)
                    receptance(a, 1)

            def first(t):
                a, c = t, back(t, 2)
                peeled_waits(a, c)
                turn_q(a)
                turn_1(a)
                set_up()
                key(a, c, 0)
                product_q(a)
                key(a, c, 1)
                value(a, c, 0)
                value(a, c, 1)
                receptance(a, 0)
                receptance(a, 1)

            def second(t):
                a, b, c = t, back(t, 1), back(t, 2)
                peeled_waits(a, c)
                turn_q(a)
                turn_1(a)
                product_q(a)
                key(a, c, 0)
                key(a, c, 1)
                value(a, c, 0)
                turn_2(a, b)
                value(a, c, 1)
                receptance(a, 0)
                turn_3(b)
                receptance(a, 1)

            def last_but_one(t):
                a, b, c = t, back(t, 1), back(t, 2)
                peeled_waits(a, c)
                gate_c(c, t, 0)
                gate_c(c, t, 1)
                hidden(c, 0, t)
                hidden(c, 1, t)
                hidden(c, 2, t)
                hidden(c, 3, t)
                hidden(c, 4, t)
                hidden(c, 5, t)
                hidden(c, 6, t)
                value_c(c, 0)
                turn_2(a, b)
                hidden(c, 7, t)
                value_c(c, 1)
                value_c(c, 2)
                value_c(c, 3)
                value_c(c, 4)
                turn_3(b)
                value_c(c, 5)
                value_c(c, 6)
                value_c(c, 7)

            def last(t):
                a, c = t, back(t, 2)
                peeled_waits(a, c)
                gate_c(c, t, 0)
                gate_c(c, t, 1)
                hidden(c, 0, t)
                hidden(c, 1, t)
                hidden(c, 2, t)
                hidden(c, 3, t)
                hidden(c, 4, t)
                hidden(c, 5, t)
                value_c(c, 0)
                value_c(c, 1)
                hidden(c, 6, t)
                hidden(c, 7, t)
                value_c(c, 2)
                value_c(c, 3)
                value_c(c, 4)
                value_c(c, 5)
                value_c(c, 6)
                value_c(c, 7)

            iterations(pe, step, {0: first, 1: second, N: last_but_one, N + 1: last})


def kernel(**inputs):
    import numpy as np
    import concourse.bacc as bacc
    from concourse.bass_utils import run_bass_kernel_spmd

    def get(name):
        return np.asarray(inputs["L0_" + name])

    vectors = {"g1": "attn_ln1_g", "b1": "attn_ln1_b", "rk": "attn_rk", "rv": "attn_rv", "rr": "attn_rr",
               "g2": "attn_ln2_g", "b2": "attn_ln2_b", "crk": "attn_crk", "crr": "attn_crr",
               "w": "attn_w", "u": "attn_u"}
    packed = np.stack([get(vectors[n]).reshape(HALF, P) for n in COLS])
    arrays = {
        "x": get("attn_x"),
        "cols": packed.transpose(2, 0, 1).reshape(P, len(COLS) * HALF),
        "wk": get("attn_Wk").T, "wv": get("attn_Wv").T, "wr": get("attn_Wr").T,
        "wcr": get("attn_Wcr").T, "wck": get("attn_Wck").T, "wcv": get("attn_Wcv").T,
        "rhs": get("ffn_rhs"),
    }
    arrays = {f"in_{n}": np.ascontiguousarray(a) for n, a in arrays.items()}
    nc = bacc.Bacc("TRN2", target_bir_lowering=False, num_devices=1)
    args = [nc.dram_tensor(n, a.shape, mybir.dt.from_np(a.dtype), kind="ExternalInput").ap() for n, a in arrays.items()]
    args.append(nc.dram_tensor("out", (B, T, C), F32, kind="ExternalOutput").ap())
    rwkv_program(nc, *args)
    r = run_bass_kernel_spmd(nc, [arrays], core_ids=[0])
    return r.results[0]["out"]
```
